# Optimizing a Trainium2 kernel written in Bass

```python
import numpy as np
import jax
import jax.numpy as jnp

def _softmax(x, axis=-1):
    return jax.nn.softmax(x, axis=axis)

def _gelu(x):
    return jax.nn.gelu(x, approximate=True)

def _silu(x):
    return jax.nn.silu(x)

def _sigmoid(x):
    return jax.nn.sigmoid(x)

def _layernorm(x, axis=-1, eps=1e-05):
    m = jnp.mean(x, axis=axis, keepdims=True)
    v = jnp.var(x, axis=axis, keepdims=True)
    return (x - m) / jnp.sqrt(v + eps)

def _scatter_add(tgt, idx, src, axis=0):
    return tgt.at[idx].add(src)

def _segment_sum(src, seg, n):
    return jax.ops.segment_sum(src, seg, n)
kernel_name = 'mk_conv_preact_d2_conv_nhwc1024_r4_ba72b6'

def setup_inputs(seed: int=0):
    np.random.seed(seed)
    _w = jnp.asarray

    def _rec_inputs():
        import jax
        import jax.numpy as jnp
        _gk = jax.random.key(seed)
        x = -0.000125 + 0.9999 * jax.random.normal(jax.random.fold_in(_gk, 1), (8, 16, 16, 256), jnp.float32)
        return x
    x = _rec_inputs()

    def _L0_conv_setup():
        import jax, jax.numpy as jnp
        import numpy as np
        HEADS = 16

        def _self_attention(x, w_qkv, w_out, heads):
            b, t, d = x.shape
            dh = d // heads
            qkv = x @ w_qkv
            q, k, v = jnp.split(qkv, 3, axis=-1)
            split = lambda z: z.reshape(b, t, heads, dh).transpose(0, 2, 1, 3)
            q, k, v = (split(q), split(k), split(v))
            dots = jnp.einsum('bhie,bhje->bhij', q, k) * d ** (-0.5)
            out = jnp.einsum('bhij,bhje->bhie', dots, v)
            out = out.transpose(0, 2, 1, 3).reshape(b, t, d)
            return out @ w_out
        key = jax.random.key(seed)
        ks = jax.random.split(key, 5)
        B, H, W, D = (8, 16, 16, 256)
        s = D ** (-0.5)
        return {'x': jax.random.normal(ks[0], (B, H, W, D), jnp.float32), 'w_qkv0': jax.random.normal(ks[1], (D, 3 * D), jnp.float32) * s, 'w_out0': jax.random.normal(ks[2], (D, D), jnp.float32) * s, 'w_qkv1': jax.random.normal(ks[3], (D, 3 * D), jnp.float32) * s, 'w_out1': jax.random.normal(ks[4], (D, D), jnp.float32) * s}
    _L0_conv_all = _L0_conv_setup()
    _L0_conv_in = {k: v for k, v in _L0_conv_all.items() if k in ('w_qkv0', 'w_out0', 'w_qkv1', 'w_out1')}
    del _L0_conv_all

    def _L1_conv_setup():
        import jax, jax.numpy as jnp
        import numpy as np
        B, H, W, D = (8, 16, 16, 256)

        def _dist(n, dtype):
            i = jnp.arange(n)
            return jnp.square(i[:, None] - i[None, :]).astype(dtype)
        key = jax.random.key(seed)
        ks = jax.random.split(key, 10)
        s = 0.02
        return {'x': jax.random.normal(ks[0], (B, H, W, D), dtype=jnp.float32), 'Wq': jax.random.normal(ks[1], (D, D), dtype=jnp.float32) * s, 'bq': jnp.zeros((D,), dtype=jnp.float32), 'Wk': jax.random.normal(ks[2], (D, D), dtype=jnp.float32) * s, 'bk': jnp.zeros((D,), dtype=jnp.float32), 'Wv': jax.random.normal(ks[3], (D, D), dtype=jnp.float32) * s, 'bv': jnp.zeros((D,), dtype=jnp.float32), 'Wo': jax.random.normal(ks[4], (D, D), dtype=jnp.float32) * s, 'bo': jnp.zeros((D,), dtype=jnp.float32), 'sigma': jnp.ones((1,), dtype=jnp.float32)}
    _L1_conv_all = _L1_conv_setup()
    _L1_conv_in = {k: v for k, v in _L1_conv_all.items() if k in ('Wq', 'bq', 'Wk', 'bk', 'Wv', 'bv', 'Wo', 'bo', 'sigma')}
    del _L1_conv_all
    return {'x': x, 'L0_conv_w_qkv0': _L0_conv_in['w_qkv0'], 'L0_conv_w_out0': _L0_conv_in['w_out0'], 'L0_conv_w_qkv1': _L0_conv_in['w_qkv1'], 'L0_conv_w_out1': _L0_conv_in['w_out1'], 'L1_conv_Wq': _L1_conv_in['Wq'], 'L1_conv_bq': _L1_conv_in['bq'], 'L1_conv_Wk': _L1_conv_in['Wk'], 'L1_conv_bk': _L1_conv_in['bk'], 'L1_conv_Wv': _L1_conv_in['Wv'], 'L1_conv_bv': _L1_conv_in['bv'], 'L1_conv_Wo': _L1_conv_in['Wo'], 'L1_conv_bo': _L1_conv_in['bo'], 'L1_conv_sigma': _L1_conv_in['sigma']}

def reference(x, L0_conv_w_qkv0, L0_conv_w_out0, L0_conv_w_qkv1, L0_conv_w_out1, L1_conv_Wq, L1_conv_bq, L1_conv_Wk, L1_conv_bk, L1_conv_Wv, L1_conv_bv, L1_conv_Wo, L1_conv_bo, L1_conv_sigma):
    import jax
    import jax.numpy as jnp

    def _L0_conv_ref(x, w_qkv0, w_out0, w_qkv1, w_out1):
        import jax, jax.numpy as jnp
        import numpy as np
        HEADS = 16

        def _self_attention(x, w_qkv, w_out, heads):
            b, t, d = x.shape
            dh = d // heads
            qkv = x @ w_qkv
            q, k, v = jnp.split(qkv, 3, axis=-1)
            split = lambda z: z.reshape(b, t, heads, dh).transpose(0, 2, 1, 3)
            q, k, v = (split(q), split(k), split(v))
            dots = jnp.einsum('bhie,bhje->bhij', q, k) * d ** (-0.5)
            out = jnp.einsum('bhij,bhje->bhie', dots, v)
            out = out.transpose(0, 2, 1, 3).reshape(b, t, d)
            return out @ w_out
        b, hh, ww, d = x.shape
        xh = x.transpose(0, 2, 1, 3).reshape(b * ww, hh, d)
        oh = _self_attention(xh, w_qkv0, w_out0, HEADS)
        oh = oh.reshape(b, ww, hh, d).transpose(0, 2, 1, 3)
        xw = x.reshape(b * hh, ww, d)
        ow = _self_attention(xw, w_qkv1, w_out1, HEADS)
        ow = ow.reshape(b, hh, ww, d)
        return oh + ow

    def _L1_conv_ref(x, Wq, bq, Wk, bk, Wv, bv, Wo, bo, sigma):
        import jax, jax.numpy as jnp
        import numpy as np
        B, H, W, D = (8, 16, 16, 256)

        def _dist(n, dtype):
            i = jnp.arange(n)
            return jnp.square(i[:, None] - i[None, :]).astype(dtype)
        b, h, w, d = x.shape
        gw = 1.0 / (2.0 * jnp.square(sigma))
        q = jnp.einsum('bhwd,ed->bhwe', x, Wq) + bq
        k = jnp.einsum('bhwd,ed->bhwe', x, Wk) + bk
        v = jnp.einsum('bhwd,ed->bhwe', x, Wv) + bv
        r_qk = jnp.einsum('bhwd,bhkd->bhwk', q, k) - gw[0] * _dist(w, x.dtype)
        r_attn = jax.nn.softmax(r_qk, axis=-1)
        r_out = jnp.einsum('bhwk,bhkd->bhwd', r_attn, v)
        c_qk = jnp.einsum('bhwd,bgwd->bwhg', q, k) - gw[0] * _dist(h, x.dtype)
        c_attn = jax.nn.softmax(c_qk, axis=-1)
        c_out = jnp.einsum('bwhg,bgwd->bhwd', c_attn, v)
        out = r_out + c_out
        return jnp.einsum('bhwd,ed->bhwe', out, Wo) + bo

    def _gn(v, G=32, eps=1e-05):
        B_, H_, W_, C_ = v.shape
        g = v.reshape(B_, H_, W_, G, C_ // G)
        m = jnp.mean(g, axis=(1, 2, 4), keepdims=True)
        s = jnp.var(g, axis=(1, 2, 4), keepdims=True)
        return ((g - m) / jnp.sqrt(s + eps)).reshape(v.shape)

    def _ln_c(v, eps=1e-06):
        m = jnp.mean(v, axis=-1, keepdims=True)
        s = jnp.var(v, axis=-1, keepdims=True)
        return (v - m) / jnp.sqrt(s + eps)

    def _ln_t(v, eps=1e-05):
        m = jnp.mean(v, axis=-1, keepdims=True)
        s = jnp.var(v, axis=-1, keepdims=True)
        return (v - m) / jnp.sqrt(s + eps)

    def _to_tokens(v):
        B_, H_, W_, C_ = v.shape
        return v.reshape(B_, H_ * W_, C_)

    def _from_tokens(t, like):
        return t.reshape(like.shape)
    x = x + _L0_conv_ref(_gn(x), L0_conv_w_qkv0, L0_conv_w_out0, L0_conv_w_qkv1, L0_conv_w_out1)
    x = x + _L1_conv_ref(_gn(x), L1_conv_Wq, L1_conv_bq, L1_conv_Wk, L1_conv_bk, L1_conv_Wv, L1_conv_bv, L1_conv_Wo, L1_conv_bo, L1_conv_sigma)
    return x

_drawn_inputs = setup_inputs


def setup_inputs(seed=0):
    import zlib

    import numpy as np

    out = dict(_drawn_inputs(seed))
    spreads = {'L1_conv_bq': (0.0, 0.448),
     'L1_conv_bk': (0.0, 0.8),
     'L1_conv_bv': (0.0, 0.1),
     'L1_conv_bo': (0.0, 0.1)}
    factors = {}
    for name, (base, spread) in spreads.items():
        noise = np.random.default_rng([zlib.crc32(name.encode()), seed]).standard_normal(out[name].shape)
        drawn = base * np.exp(spread * noise) if base else spread * noise
        out[name] = jnp.asarray(drawn.astype(out[name].dtype))
    for name, factor in factors.items():
        out[name] = (out[name] * factor).astype(out[name].dtype)
    return out
```

```python
import concourse.bass as bass
from concourse import mybir
from contextlib import ExitStack

FP32 = mybir.dt.float32
FP32R = mybir.dt.float32r
INT32 = mybir.dt.int32
ALU = mybir.AluOpType
ACT = mybir.ActivationFunctionType
AX = mybir.AxisListType

BATCHES, SIDE, DIM = 8, 16, 256
TOKENS = SIDE * SIDE
P = 128
TT = TOKENS // P
CC = DIM // P
HEAD = 16
GROUP = 8
EPS = 1e-5
QUAD = 32
QUADS = P // QUAD
BLOCKS = 2 * TT * QUADS
LAG = 4
SLOTS = 4
BANKS = 3
FAR = 1.0e30
POOL_LO = [n for n in range(BLOCKS) if n % 4 != 3]
DVE_LO = [n for n in range(BLOCKS) if n % 4 == 3]


def block_of(n):
    return n // (TT * QUADS), n // QUADS % TT, n % QUADS


def build(nc, x, w_qkv0, w_out0, w_qkv1, w_out1, wq, bq, wk, bk, wv, bv, wo, bo, sigma, out):
    with ExitStack() as ctx:
        def sb(name, shape, dt=FP32):
            return ctx.enter_context(nc.sbuf_tensor(name, shape, dt))

        def sem(name):
            return ctx.enter_context(nc.semaphore(name))

        wqkv_in = sb("wqkv_in", [P, 2, CC, 3 * DIM])
        wqkv_hi = sb("wqkv_hi", [P, 2, CC, 3 * DIM], FP32R)
        wqkv_lo = sb("wqkv_lo", [P, 2, CC, 3 * DIM], FP32R)
        wout_in = sb("wout_in", [P, 2, CC, DIM])
        wout_hi = sb("wout_hi", [P, 2, CC, DIM], FP32R)
        wout_lo = sb("wout_lo", [P, 2, CC, DIM], FP32R)
        wl1 = sb("wl1", [P, 4, CC, DIM])
        wo_t = sb("wo_t", [P, CC, DIM])
        g_hi = sb("g_hi", [P, CC, DIM], FP32R)
        g_lo = sb("g_lo", [P, CC, DIM], FP32R)
        wvo_hi = sb("wvo_hi", [P, CC, DIM], FP32R)
        wvo_lo = sb("wvo_lo", [P, CC, DIM], FP32R)
        bias_in = sb("bias_in", [P, 3, CC])
        bq_rep = sb("bq_rep", [P, CC, P])
        bv2_rep = sb("bv2_rep", [P, CC, P])
        bo_row = sb("bo_row", [P, DIM])
        bias_out = sb("bias_out", [P, DIM])
        c1 = sb("c1", [P, CC])
        r_col = sb("r_col", [P, CC])
        s0 = sb("s0", [P, 1])
        sig = sb("sig", [P, 1])
        neg_gw = sb("neg_gw", [P, 1])
        iota_row = sb("iota_row", [P, 1], INT32)
        iota_j = sb("iota_j", [P, 4, TOKENS], INT32)
        ji = sb("ji", [P, 4, TOKENS])
        part_i = sb("part_i", [P, 4], INT32)
        pi = sb("pi", [P, 4])
        par_i = sb("par_i", [P, 1], INT32)
        parity = sb("parity", [P, 2])
        ident = sb("ident", [P, P])
        group_avg = sb("group_avg", [P, P])
        head_mask = sb("head_mask", [P, 4, P])
        row_mask = sb("row_mask", [P, P])
        col_mask = sb("col_mask", [P, TT, TOKENS])
        hcol = sb("hcol", [P, TT])
        scratch = sb("scratch", [P, 2, TOKENS])
        gate = sb("gate", [P, 1])
        minus_half = sb("minus_half", [P, CC])
        x_in = sb("x_in", [P, TT, DIM])
        x_res = sb("x_res", [P, TT, DIM])
        moments = [sb(f"moments{k}", [P, CC, 6]) for k in range(2)]
        mv = [sb(f"mv{k}", [P, CC, 2]) for k in range(2)]
        gmean = [sb(f"gmean{k}", [P, CC]) for k in range(2)]
        shift = [sb(f"shift{k}", [P, 2, CC]) for k in range(2)]
        var_eps = [sb(f"var_eps{k}", [P, CC]) for k in range(2)]
        rstd = [sb(f"rstd{k}", [P, CC]) for k in range(2)]
        nbias = [sb(f"nbias{k}", [P, CC]) for k in range(2)]
        xn = [sb(f"xn{k}", [P, CC, TOKENS]) for k in range(2)]
        xn_hi = [sb(f"xn_hi{k}", [P, CC, TOKENS], FP32R) for k in range(2)]
        xn_lo = [sb(f"xn_lo{k}", [P, CC, TOKENS], FP32R) for k in range(2)]
        xt_hi = sb("xt_hi", [P, CC, TOKENS], FP32R)
        xt_lo = sb("xt_lo", [P, CC, TOKENS], FP32R)
        k_hi = sb("k_hi", [P, 2, TT, DIM], FP32R)
        k_lo = sb("k_lo", [P, 2, TT, DIM], FP32R)
        v_hi = sb("v_hi", [P, 2, TT, 2, DIM], FP32R)
        v_lo = sb("v_lo", [P, 2, TT, 2, DIM], FP32R)
        q_hi = sb("q_hi", [P, 2, CC, TOKENS], FP32R)
        q_lo = sb("q_lo", [P, 2, CC, TOKENS], FP32R)
        kv = sb("kv", [P, SLOTS, 4 * P])
        kv_hi = sb("kv_hi", [P, SLOTS, CC, 2, P], FP32R)
        kv_lo = sb("kv_lo", [P, SLOTS, CC, 2, P], FP32R)
        o_hi = sb("o_hi", [P, 2, CC, TOKENS], FP32R)
        o_lo = sb("o_lo", [P, 2, CC, TOKENS], FP32R)
        x1 = sb("x1", [P, TT, DIM])
        x1b = sb("x1b", [P, TT, DIM])
        t_hi = sb("t_hi", [P, CC, TOKENS], FP32R)
        t_lo = sb("t_lo", [P, CC, TOKENS], FP32R)
        vp_hi = sb("vp_hi", [P, TT, DIM], FP32R)
        vp_lo = sb("vp_lo", [P, TT, DIM], FP32R)
        row_term = sb("row_term", [P, TT])
        log_row = sb("log_row", [P, TT, P])
        log_col = sb("log_col", [P, TT, TOKENS])
        neg_max = sb("neg_max", [P, 2, TT])
        exp_row = sb("exp_row", [P, TT, P])
        exp_col = sb("exp_col", [P, TT, TOKENS])
        exp_sum = sb("exp_sum", [P, 2, TT])
        inv_sum = sb("inv_sum", [P, 2, TT])
        attn = sb("attn", [P, TT, TOKENS])
        at_hi = sb("at_hi", [P, TT, TT, P], FP32R)
        at_lo = sb("at_lo", [P, TT, TT, P], FP32R)
        y_out = sb("y_out", [P, TT, DIM])
        bank = [ctx.enter_context(nc.psum_tensor(f"bank{i}", [P, 512], FP32)) for i in range(8)]
        trans_bank, stat_bank, y_bank = bank[0], bank[1], bank[7]
        ring = bank[2:2 + BANKS]
        o_bank = bank[5:7]

        x_loaded, stored = sem("x_loaded"), sem("stored")
        w_loaded = [sem(f"w_loaded{i}") for i in range(2)]
        wout_loaded, l1_loaded, bias_loaded = sem("wout_loaded"), sem("l1_loaded"), sem("bias_loaded")
        iota_done, const_step, consts_ready = sem("iota_done"), sem("const_step"), sem("consts_ready")
        w_hi_done, w_split = sem("w_hi_done"), sem("w_split")
        fold_ready, fold_hi_done, fold_split = sem("fold_ready"), sem("fold_hi_done"), sem("fold_split")
        wot_ready, wot_done, bias_step = sem("wot_ready"), sem("wot_done"), sem("bias_step")
        xt_ready = [sem(f"xt_ready{k}") for k in range(2)]
        norm_step = [sem(f"norm_step{k}") for k in range(2)]
        stat_in = [sem(f"stat_in{k}") for k in range(2)]
        stat_sum = [sem(f"stat_sum{k}") for k in range(2)]
        var_ready = [sem(f"var_ready{k}") for k in range(2)]
        rstd_ready = [sem(f"rstd_ready{k}") for k in range(2)]
        coef_ready = [sem(f"coef_ready{k}") for k in range(2)]
        xn_ready = [sem(f"xn_ready{k}") for k in range(2)]
        xn_hi_done = [sem(f"xn_hi_done{k}") for k in range(2)]
        xn_split = [sem(f"xn_split{k}") for k in range(2)]
        res_ready, turned = sem("res_ready"), sem("turned")
        kv_proj, kv_hi_done, kv_lo_done = sem("kv_proj"), sem("kv_hi_done"), sem("kv_lo_done")
        q_proj, q_hi_done, q_lo_done = sem("q_proj"), sem("q_hi_done"), sem("q_lo_done")
        blk_ready, blk_masked, blk_hi = sem("blk_ready"), sem("blk_masked"), sem("blk_hi")
        blk_lo_pool, blk_lo_dve, blk_used = sem("blk_lo_pool"), sem("blk_lo_dve"), sem("blk_used")
        o_hi_done, o_lo_done = sem("o_hi_done"), sem("o_lo_done")
        y_ready, x1_ready, x1b_ready = sem("y_ready"), sem("x1_ready"), sem("x1b_ready")
        t_ready, t_hi_done, t_lo_done = sem("t_ready"), sem("t_hi_done"), sem("t_lo_done")
        row_ready, row_done = sem("row_ready"), sem("row_done")
        vp_ready, vp_hi_done, vp_lo_done = sem("vp_ready"), sem("vp_hi_done"), sem("vp_lo_done")
        s_ready, logits_done, max_ready = sem("s_ready"), sem("logits_done"), sem("max_ready")
        exp_done, soft_step, attn_ready = sem("exp_done"), sem("soft_step"), sem("attn_ready")
        at_ready, at_hi_done, at_lo_done = sem("at_ready"), sem("at_hi_done"), sem("at_lo_done")
        pv_ready, out_ready = sem("pv_ready"), sem("out_ready")

        x_dram = x.rearrange("b h w d -> b (h w) d")
        out_dram = out.rearrange("b h w d -> b (h w) d")

        def by_axis(ap, axis):
            return ap.rearrange("p (h w) -> p w h", h=SIDE) if axis == 0 else ap.rearrange("p (h w) -> p h w", h=SIDE)

        block = ctx.enter_context(nc.Block())

        @block.sync
        def _(sp):
            def load_x(b):
                sp.dma_start(x_in[:, :, :], x_dram[bass.ds(b, 1), :, :].rearrange("a (t p) d -> p (a t) d", p=P)
                             ).then_inc(x_loaded, 16)

            def store_y(b):
                sp.wait_ge(out_ready, b + 1)
                sp.dma_start(out_dram[bass.ds(b, 1), :, :].rearrange("a (t p) d -> p (a t) d", p=P), y_out[:, :, :]
                             ).then_inc(stored, 16)

            load_x(0)
            sp.dma_start(wqkv_in[:, 1, :, :], w_qkv1.rearrange("(c p) n -> p c n", p=P)).then_inc(w_loaded[1], 16)
            sp.dma_start(wout_in[:, 0, :, :], w_out0.rearrange("(c p) n -> p c n", p=P)).then_inc(wout_loaded, 16)
            for i, w in enumerate((wq, wk)):
                sp.dma_start(wl1[:, i, :, :], w.rearrange("(c p) n -> p c n", p=P)).then_inc(l1_loaded, 16)

            def batch(b, has_prev, has_next):
                if has_next:
                    sp.wait_ge(xt_ready[0], b + 1)
                    sp.wait_ge(res_ready, b + 1)
                    load_x(b + 1)
                if has_prev:
                    store_y(b - 1)

            batch(0, False, True)
            with sp.Fori(1, BATCHES - 1) as b:
                batch(b, True, True)
            batch(BATCHES - 1, True, False)
            store_y(BATCHES - 1)
            sp.wait_ge(stored, 16 * BATCHES)

        @block.gpsimd
        def _(pool):
            pool.iota(iota_row[:, :], [[0, 1]], base=0, channel_multiplier=1).then_inc(iota_done, 1)
            for i, pattern in enumerate(([[1, 256]], [[1, 16], [0, 16]], [[0, 16], [1, 16]], [[1, 32], [0, 8]])):
                pool.iota(iota_j[:, i, :], pattern, base=0, channel_multiplier=0).then_inc(iota_done, 1)

            def turn(b):
                if not (isinstance(b, int) and b == 0):
                    pool.wait_ge(q_proj, 2 * b)
                pool.wait_ge(xn_hi_done[0], b + 1)
                for c in range(CC):
                    pool.tensor_tensor(xt_lo[:, c, :].rearrange("p (w h) -> p w h", w=SIDE), by_axis(xn[0][:, c, :], 0),
                                       by_axis(xn_hi[0][:, c, :].bitcast(FP32), 0), ALU.subtract)
                for c in range(CC):
                    last = pool.tensor_copy(xt_hi[:, c, :].rearrange("p (w h) -> p w h", w=SIDE), by_axis(xn_hi[0][:, c, :], 0))
                last.then_inc(turned, 1)

            def inverse_root(k, b):
                pool.wait_ge(var_ready[k], b + 1)
                pool.tensor_tensor(rstd[k][:, :], var_eps[k][:, :], minus_half[:, :], ALU.pow).then_inc(rstd_ready[k], 1)

            pool.memset(minus_half[:, :], -0.5).then_inc(iota_done, 1)
            pool.wait_ge(iota_done, 6)
            inverse_root(0, 0)
            turn(0)

            def batch(b, has_next):
                for n in POOL_LO:
                    pool.wait_ge(blk_hi, BLOCKS * b + n + 1)
                    pool.tensor_tensor(kv_lo[:, n % SLOTS, :, :, :].rearrange("p c s e -> p (c s e)"), kv[:, n % SLOTS, :],
                                       kv_hi[:, n % SLOTS, :, :, :].rearrange("p c s e -> p (c s e)").bitcast(FP32),
                                       ALU.subtract).then_inc(blk_lo_pool, 1)
                if has_next:
                    inverse_root(0, b + 1)
                    turn(b + 1)
                pool.wait_ge(x1_ready, b + 1)
                pool.wait_ge(out_ready, b)
                for t in range(TT):
                    last = pool.tensor_tensor(x1b[:, t, :], x1[:, t, :], bias_out[:, :], ALU.add)
                last.then_inc(x1b_ready, 1)
                inverse_root(1, b)

            pool.wait_ge(bias_step, 5)
            batch(0, True)
            with pool.Fori(1, BATCHES - 1) as b:
                batch(b, True)
            batch(BATCHES - 1, False)

        @block.scalar
        def _(act):
            act.dma_start(sig[:, :], sigma.rearrange("(a n) -> a n", a=1).partition_broadcast(P)).then_inc(bias_loaded, 16)
            act.dma_start(wqkv_in[:, 0, :, :], w_qkv0.rearrange("(c p) n -> p c n", p=P)).then_inc(w_loaded[0], 16)
            act.dma_start(wout_in[:, 1, :, :], w_out1.rearrange("(c p) n -> p c n", p=P)).then_inc(wout_loaded, 16)
            for i, w in ((2, wv), (3, wo)):
                act.dma_start(wl1[:, i, :, :], w.rearrange("(c p) n -> p c n", p=P)).then_inc(l1_loaded, 16)
            for i, v in enumerate((bq, bk, bv)):
                act.dma_start(bias_in[:, i, :], v.rearrange("(c p) -> p c", p=P), allow_slow_non_contiguous=True).then_inc(bias_loaded, 16)
            act.dma_start(bo_row[:, :], bo.rearrange("(a n) -> a n", a=1).partition_broadcast(P)).then_inc(bias_loaded, 16)

            def copy_residual(b):
                act.wait_ge(x_loaded, 16 * (b + 1))
                act.wait_ge(x1_ready, b)
                act.activation(x_res[:, :, :], x_in[:, :, :], ACT.Copy).then_inc(res_ready, 1)

            def normalise(k, b):
                act.wait_ge(coef_ready[k], b + 1)
                act.wait_ge(xn_split[k], b)
                if k == 0:
                    act.wait_ge(turned, b)
                for c in range(CC):
                    last = act.activation(xn[k][:, c, :], trans_bank[:, c * TOKENS:(c + 1) * TOKENS], ACT.Identity,
                                          bias=nbias[k][:, c:c + 1], scale=rstd[k][:, c:c + 1])
                last.then_inc(xn_ready[k], 1)

            def split_kv(b, i):
                axis, t = 1 - i // TT, i % TT
                src = ring[i % BANKS]
                act.wait_ge(kv_proj, 4 * b + i + 1)
                act.activation(k_hi[:, axis, t, :], src[:, 0:DIM], ACT.Copy)
                for s in range(2):
                    last = act.activation(v_hi[:, axis, t, s, :], src[:, DIM:2 * DIM], ACT.Copy, scale=parity[:, s:s + 1])
                last.then_inc(kv_hi_done, 1)

            def split_q(b, i):
                act.wait_ge(q_proj, 2 * b + i + 1)
                act.activation(q_hi[:, 1 - i, :, :].rearrange("p c n -> p (c n)"), ring[1 + i][:, :], ACT.Copy).then_inc(q_hi_done, 1)

            def split_o(b, axis):
                act.wait_ge(blk_used, BLOCKS * b + TT * QUADS * (axis + 1))
                for c in range(CC):
                    last = act.activation(by_axis(o_hi[:, axis, c, :], axis),
                                          o_bank[axis][:, c * TOKENS:(c + 1) * TOKENS].rearrange("p (s i) -> p s i", s=SIDE), ACT.Copy)
                last.then_inc(o_hi_done, 1)

            def exponentials(b):
                act.wait_ge(max_ready, b + 1)
                for t in range(TT):
                    act.activation(exp_row[:, t, :], log_row[:, t, :], ACT.Exp, bias=neg_max[:, 0, t:t + 1],
                                   accum_out=exp_sum[:, 0, t:t + 1])
                    last = act.activation(exp_col[:, t, :], log_col[:, t, :], ACT.Exp, bias=neg_max[:, 1, t:t + 1],
                                          accum_out=exp_sum[:, 1, t:t + 1])
                last.then_inc(exp_done, 1)

            def split_attn(b):
                act.wait_ge(at_ready, b + 1)
                act.activation(at_hi[:, :, :, :].rearrange("p j i q -> p (j i q)"), trans_bank[:, :], ACT.Copy).then_inc(at_hi_done, 1)

            def attention(b, has_prev, has_next):
                for n in range(BLOCKS):
                    act.wait_ge(blk_masked, BLOCKS * b + n + 1)
                    act.activation(kv_hi[:, n % SLOTS, :, :, :].rearrange("p c s e -> p (c s e)"), kv[:, n % SLOTS, :],
                                   ACT.Copy).then_inc(blk_hi, 1)
                    if n == 0 and has_prev:
                        exponentials(b - 1)
                    if n == 5 and has_prev:
                        split_attn(b - 1)
                    if n == 11:
                        split_o(b, 0)
                if has_next:
                    normalise(0, b + 1)
                split_o(b, 1)

            def project(b, has_next):
                if has_next:
                    for i in range(2 * TT):
                        split_kv(b + 1, i)
                        if i == 1:
                            copy_residual(b + 1)
                    split_q(b + 1, 0)
                normalise(1, b)
                if has_next:
                    split_q(b + 1, 1)
                act.wait_ge(t_ready, b + 1)
                for c in range(CC):
                    last = act.activation(t_hi[:, c, :], o_bank[0][:, c * TOKENS:(c + 1) * TOKENS], ACT.Identity, bias=c1[:, c:c + 1])
                last.then_inc(t_hi_done, 1)
                act.wait_ge(vp_ready, b + 1)
                act.activation(vp_hi[:, :, :].rearrange("p t d -> p (t d)"), o_bank[1][:, :], ACT.Copy).then_inc(vp_hi_done, 1)

            copy_residual(0)
            act.wait_ge(consts_ready, 1)
            for axis in (1, 0):
                act.wait_ge(w_loaded[axis], 16)
                act.activation(wqkv_hi[:, axis, :, 0:DIM], wqkv_in[:, axis, :, 0:DIM], ACT.Copy, scale=DIM ** -0.5)
                act.activation(wqkv_hi[:, axis, :, DIM:3 * DIM], wqkv_in[:, axis, :, DIM:3 * DIM], ACT.Copy).then_inc(w_hi_done, 1)
                if axis == 1:
                    normalise(0, 0)
            act.wait_ge(wout_loaded, 32)
            act.activation(wout_hi[:, :, :, :].rearrange("p a c n -> p (a c n)"),
                           wout_in[:, :, :, :].rearrange("p a c n -> p (a c n)"), ACT.Copy).then_inc(w_hi_done, 1)
            for i in range(2 * TT):
                split_kv(0, i)
            for i in range(2):
                split_q(0, i)
            for i, (dst, src) in enumerate(((g_hi, y_bank), (wvo_hi, o_bank[1]))):
                act.wait_ge(fold_ready, i + 1)
                act.activation(dst[:, :, :].rearrange("p c n -> p (c n)"), src[:, :], ACT.Copy).then_inc(fold_hi_done, 1)

            attention(0, False, True)
            project(0, True)
            with act.Fori(1, BATCHES - 1) as b:
                attention(b, True, True)
                project(b, True)
            attention(BATCHES - 1, True, False)
            project(BATCHES - 1, False)
            exponentials(BATCHES - 1)
            split_attn(BATCHES - 1)

        @block.vector
        def _(dve):
            steps = [0]

            def const(inst):
                inst.then_inc(const_step, 1)
                steps[0] += 1
                dve.wait_ge(const_step, steps[0])

            dve.wait_ge(iota_done, 5)
            const(dve.tensor_copy(ji[:, :, :], iota_j[:, :, :]))
            for i, (shift_by, keep) in enumerate(((0, 0x7f), (4, 0x7f), (0, 15), (3, 0x7f))):
                dve.tensor_scalar(part_i[:, i:i + 1], iota_row[:, :], shift_by, keep, ALU.logical_shift_right, ALU.bitwise_and)
            const(dve.tensor_scalar(par_i[:, :], iota_row[:, :], 4, 1, ALU.logical_shift_right, ALU.bitwise_and))
            const(dve.tensor_copy(pi[:, :], part_i[:, :]))
            dve.tensor_scalar(ident[:, :], ji[:, 0, 0:P], pi[:, 0:1], None, ALU.is_equal)
            dve.tensor_scalar(group_avg[:, :], ji[:, 3, 0:P], pi[:, 3:4], 1.0 / GROUP, ALU.is_equal, ALU.mult)
            for i in range(4):
                dve.tensor_scalar(head_mask[:, i, :], ji[:, 1, 0:P], pi[:, 1:2], None, ALU.is_equal)
            const(dve.tensor_copy(parity[:, 1:2], par_i[:, :]))
            dve.tensor_scalar(parity[:, 0:1], parity[:, 1:2], -1.0, 1.0, ALU.mult, ALU.add).then_inc(consts_ready, 1)

            def statistics(k, b):
                dve.wait_ge(xt_ready[k], b + 1)
                for c in range(CC):
                    last = dve.bn_stats(moments[k][:, c, :], trans_bank[:, c * TOKENS:(c + 1) * TOKENS])
                last.then_inc(norm_step[k], 1)
                dve.wait_ge(norm_step[k], 4 * b + 1)
                dve.memset(gate[:, :], 0.0)
                for c in range(CC):
                    last = dve.bn_aggr(mv[k][:, c, :], moments[k][:, c, :])
                last.then_inc(stat_in[k], 1)

            def spread(k, b):
                dve.wait_ge(stat_sum[k], 2 * b + 1)
                dve.tensor_copy(gmean[k][:, :], stat_bank[:, 0:CC]).then_inc(norm_step[k], 1)
                dve.wait_ge(norm_step[k], 4 * b + 2)
                dve.tensor_tensor(shift[k][:, 0, :], mv[k][:, :, 0], gmean[k][:, :], ALU.subtract).then_inc(norm_step[k], 1)
                dve.wait_ge(norm_step[k], 4 * b + 3)
                dve.tensor_tensor(shift[k][:, 1, :], shift[k][:, 0, :], shift[k][:, 0, :], ALU.mult).then_inc(norm_step[k], 1)
                dve.wait_ge(norm_step[k], 4 * b + 4)
                dve.tensor_tensor(shift[k][:, 0, :], shift[k][:, 1, :], mv[k][:, :, 1], ALU.add).then_inc(stat_in[k], 1)

            def variance(k, b):
                dve.wait_ge(stat_sum[k], 2 * b + 2)
                dve.tensor_scalar(var_eps[k][:, :], stat_bank[:, CC:2 * CC], EPS, None, ALU.add).then_inc(var_ready[k], 1)

            def coefficients(k, b):
                dve.wait_ge(rstd_ready[k], b + 1)
                dve.scalar_tensor_tensor(nbias[k][:, :], gmean[k][:, :], -1.0, rstd[k][:, :], ALU.mult, ALU.mult).then_inc(coef_ready[k], 1)

            def split_xn(k, b):
                dve.wait_ge(xn_ready[k], b + 1)
                dve.tensor_copy(xn_hi[k][:, :, :], xn[k][:, :, :]).then_inc(xn_hi_done[k], 1)
                dve.wait_ge(xn_hi_done[k], b + 1)
                dve.tensor_tensor(xn_lo[k][:, :, :], xn[k][:, :, :], xn_hi[k][:, :, :].bitcast(FP32), ALU.subtract).then_inc(xn_split[k], 1)

            def split_kv(b, i):
                axis, t = 1 - i // TT, i % TT
                src = ring[i % BANKS]
                dve.wait_ge(kv_hi_done, 4 * b + i + 1)
                dve.tensor_tensor(k_lo[:, axis, t, :], src[:, 0:DIM], k_hi[:, axis, t, :].bitcast(FP32), ALU.subtract)
                for s in range(2):
                    last = dve.scalar_tensor_tensor(v_lo[:, axis, t, s, :], src[:, DIM:2 * DIM], parity[:, s:s + 1],
                                                    v_hi[:, axis, t, s, :].bitcast(FP32), ALU.mult, ALU.subtract)
                last.then_inc(kv_lo_done, 1)

            def split_q(b, i):
                dve.wait_ge(q_hi_done, 2 * b + i + 1)
                dve.tensor_tensor(q_lo[:, 1 - i, :, :].rearrange("p c n -> p (c n)"), ring[1 + i][:, :],
                                  q_hi[:, 1 - i, :, :].rearrange("p c n -> p (c n)").bitcast(FP32), ALU.subtract).then_inc(q_lo_done, 1)

            def split_o(b, axis):
                dve.wait_ge(o_hi_done, 2 * b + axis + 1)
                for c in range(CC):
                    last = dve.tensor_tensor(by_axis(o_lo[:, axis, c, :], axis),
                                             o_bank[axis][:, c * TOKENS:(c + 1) * TOKENS].rearrange("p (s i) -> p s i", s=SIDE),
                                             by_axis(o_hi[:, axis, c, :].bitcast(FP32), axis), ALU.subtract)
                last.then_inc(o_lo_done, 1)

            def logits(b):
                dve.wait_ge(row_done, b + 1)
                dve.wait_ge(s_ready, b + 1)
                for t in range(TT):
                    dve.scalar_tensor_tensor(log_row[:, t, :], y_bank[:, t * TOKENS + t * P:t * TOKENS + (t + 1) * P],
                                             row_term[:, t:t + 1], row_mask[:, :], ALU.add, ALU.add)
                    last = dve.scalar_tensor_tensor(log_col[:, t, :], y_bank[:, t * TOKENS:(t + 1) * TOKENS],
                                                    row_term[:, t:t + 1], col_mask[:, t, :], ALU.add, ALU.add)
                last.then_inc(logits_done, 1)

            def maxima(b):
                dve.wait_ge(logits_done, b + 1)
                dve.tensor_reduce(neg_max[:, 0, :], log_row[:, :, :], AX.X, ALU.max, negate=True)
                dve.tensor_reduce(neg_max[:, 1, :], log_col[:, :, :], AX.X, ALU.max, negate=True).then_inc(max_ready, 1)

            def weights(b):
                dve.wait_ge(exp_done, b + 1)
                dve.reciprocal(inv_sum[:, :, :], exp_sum[:, :, :]).then_inc(soft_step, 1)
                dve.wait_ge(soft_step, 2 * b + 1)
                for t in range(TT):
                    last = dve.tensor_scalar(attn[:, t, :], exp_col[:, t, :], inv_sum[:, 1, t:t + 1], None, ALU.mult)
                last.then_inc(soft_step, 1)
                dve.wait_ge(soft_step, 2 * b + 2)
                for t in range(TT):
                    own = attn[:, t, t * P:(t + 1) * P]
                    last = dve.scalar_tensor_tensor(own, exp_row[:, t, :], inv_sum[:, 0, t:t + 1], own, ALU.mult, ALU.add)
                last.then_inc(attn_ready, 1)

            def split_attn(b):
                dve.wait_ge(at_hi_done, b + 1)
                dve.tensor_tensor(at_lo[:, :, :, :].rearrange("p j i q -> p (j i q)"), trans_bank[:, :],
                                  at_hi[:, :, :, :].rearrange("p j i q -> p (j i q)").bitcast(FP32), ALU.subtract).then_inc(at_lo_done, 1)

            def final_sum(b):
                dve.wait_ge(pv_ready, b + 1)
                dve.wait_ge(x1b_ready, b + 1)
                dve.wait_ge(stored, 16 * b)
                dve.tensor_tensor(y_out[:, :, :].rearrange("p t d -> p (t d)"), y_bank[:, :],
                                  x1b[:, :, :].rearrange("p t d -> p (t d)"), ALU.add).then_inc(out_ready, 1)

            def low_block(b, n):
                dve.wait_ge(blk_hi, BLOCKS * b + n + 1)
                dve.tensor_tensor(kv_lo[:, n % SLOTS, :, :, :].rearrange("p c s e -> p (c s e)"), kv[:, n % SLOTS, :],
                                  kv_hi[:, n % SLOTS, :, :, :].rearrange("p c s e -> p (c s e)").bitcast(FP32),
                                  ALU.subtract).then_inc(blk_lo_dve, 1)

            def attention(b, has_prev, has_next):
                if has_prev:
                    logits(b - 1)
                for n in range(BLOCKS):
                    dve.wait_ge(blk_ready, BLOCKS * b + n + 1)
                    if n >= SLOTS:
                        dve.wait_ge(blk_used, BLOCKS * b + n - SLOTS + 1)
                    dve.tensor_tensor(kv[:, n % SLOTS, :], ring[n % BANKS][:, :],
                                      head_mask[:, :, :].rearrange("p a e -> p (a e)"), ALU.mult).then_inc(blk_masked, 1)
                    if n - 1 in DVE_LO:
                        low_block(b, n - 1)
                    if has_prev and n == 0:
                        maxima(b - 1)
                    if has_prev and n == 3:
                        weights(b - 1)
                    if has_prev and n == 6:
                        split_attn(b - 1)
                    if has_prev and n == 8:
                        final_sum(b - 1)
                    if has_next and n == 9:
                        statistics(0, b + 1)
                    if has_next and n == 12:
                        spread(0, b + 1)
                    if n == 13:
                        split_o(b, 0)
                    if has_next and n == 14:
                        variance(0, b + 1)
                low_block(b, BLOCKS - 1)
                if has_next:
                    coefficients(0, b + 1)
                    split_xn(0, b + 1)
                split_o(b, 1)

            def project(b, has_next):
                dve.wait_ge(y_ready, b + 1)
                dve.wait_ge(res_ready, b + 1)
                dve.wait_ge(x1b_ready, b)
                dve.tensor_tensor(x1[:, :, :].rearrange("p t d -> p (t d)"), y_bank[:, :],
                                  x_res[:, :, :].rearrange("p t d -> p (t d)"), ALU.add).then_inc(x1_ready, 1)
                if has_next:
                    split_kv(b + 1, 0)
                    split_kv(b + 1, 1)
                statistics(1, b)
                if has_next:
                    split_kv(b + 1, 2)
                spread(1, b)
                if has_next:
                    split_kv(b + 1, 3)
                variance(1, b)
                if has_next:
                    split_q(b + 1, 0)
                coefficients(1, b)
                split_xn(1, b)
                if has_next:
                    split_q(b + 1, 1)
                dve.wait_ge(t_hi_done, b + 1)
                for c in range(CC):
                    last = dve.scalar_tensor_tensor(t_lo[:, c, :], o_bank[0][:, c * TOKENS:(c + 1) * TOKENS], c1[:, c:c + 1],
                                                    t_hi[:, c, :].bitcast(FP32), ALU.add, ALU.subtract)
                last.then_inc(t_lo_done, 1)
                dve.wait_ge(row_ready, b + 1)
                dve.tensor_scalar(row_term[:, :], stat_bank[:, 2 * CC:2 * CC + TT], s0[:, :], None, ALU.add).then_inc(row_done, 1)
                dve.wait_ge(vp_hi_done, b + 1)
                dve.tensor_tensor(vp_lo[:, :, :].rearrange("p t d -> p (t d)"), o_bank[1][:, :],
                                  vp_hi[:, :, :].rearrange("p t d -> p (t d)").bitcast(FP32), ALU.subtract).then_inc(vp_lo_done, 1)

            statistics(0, 0)
            spread(0, 0)
            variance(0, 0)
            coefficients(0, 0)
            split_xn(0, 0)

            def low_qkv(axis):
                dve.wait_ge(w_hi_done, 2 - axis)
                dve.scalar_tensor_tensor(wqkv_lo[:, axis, :, 0:DIM], wqkv_in[:, axis, :, 0:DIM], DIM ** -0.5,
                                         wqkv_hi[:, axis, :, 0:DIM].bitcast(FP32), ALU.mult, ALU.subtract)
                dve.tensor_tensor(wqkv_lo[:, axis, :, DIM:3 * DIM], wqkv_in[:, axis, :, DIM:3 * DIM],
                                  wqkv_hi[:, axis, :, DIM:3 * DIM].bitcast(FP32), ALU.subtract).then_inc(w_split, 1)

            low_qkv(1)
            low_qkv(0)
            dve.wait_ge(w_hi_done, 3)
            dve.tensor_tensor(wout_lo[:, :, :, :].rearrange("p a c n -> p (a c n)"), wout_in[:, :, :, :].rearrange("p a c n -> p (a c n)"),
                              wout_hi[:, :, :, :].rearrange("p a c n -> p (a c n)").bitcast(FP32), ALU.subtract).then_inc(w_split, 1)
            dve.wait_ge(bias_loaded, 5 * 16)
            dve.memset(scratch[:, 0, 0:P], 1.0).then_inc(bias_step, 1)
            dve.wait_ge(bias_step, 1)
            for c in range(CC):
                dve.tensor_scalar(bq_rep[:, c, :], scratch[:, 0, 0:P], bias_in[:, 0, c:c + 1], None, ALU.mult)
                last = dve.tensor_scalar(bv2_rep[:, c, :], scratch[:, 0, 0:P], bias_in[:, 2, c:c + 1], 2.0, ALU.mult, ALU.mult)
            last.then_inc(bias_step, 1)
            const(dve.tensor_tensor(neg_gw[:, :], sig[:, :], sig[:, :], ALU.mult))
            const(dve.tensor_scalar(neg_gw[:, :], neg_gw[:, :], -2.0, None, ALU.mult))
            dve.reciprocal(neg_gw[:, :], neg_gw[:, :])
            for t in range(TT):
                last = dve.tensor_scalar(hcol[:, t:t + 1], pi[:, 1:2], float(t * SIDE // TT), None, ALU.add)
            const(last)
            masks = [(row_mask[:, :], P, 2, pi[:, 2:3], 1, pi[:, 1:2])]
            masks += [(col_mask[:, t, :], TOKENS, 1, hcol[:, t:t + 1], 2, pi[:, 2:3]) for t in range(TT)]
            for mask, width, along, mine, across, same in masks:
                inside, dist = scratch[:, 0, 0:width], scratch[:, 1, 0:width]
                dve.tensor_scalar(dist, ji[:, along, 0:width], mine, None, ALU.subtract)
                const(dve.tensor_scalar(inside, ji[:, across, 0:width], same, None, ALU.is_equal))
                const(dve.tensor_tensor(dist, dist, inside, ALU.mult))
                const(dve.tensor_tensor(dist, dist, dist, ALU.mult))
                dve.tensor_scalar(inside, inside, -1.0, FAR, ALU.add, ALU.mult)
                const(dve.tensor_scalar(dist, dist, neg_gw[:, :], None, ALU.mult))
                const(dve.tensor_tensor(mask, dist, inside, ALU.add))
            for i in range(2 * TT):
                split_kv(0, i)
            for i in range(2):
                split_q(0, i)
            dve.wait_ge(wot_ready, 1)
            dve.tensor_copy(wo_t[:, :, :].rearrange("p c n -> p (c n)"), trans_bank[:, :]).then_inc(wot_done, 1)
            for i, (lo, hi, src) in enumerate(((g_lo, g_hi, y_bank), (wvo_lo, wvo_hi, o_bank[1]))):
                dve.wait_ge(fold_hi_done, i + 1)
                dve.tensor_tensor(lo[:, :, :].rearrange("p c n -> p (c n)"), src[:, :],
                                  hi[:, :, :].rearrange("p c n -> p (c n)").bitcast(FP32), ALU.subtract).then_inc(fold_split, 1)
            dve.wait_ge(fold_ready, 3)
            dve.tensor_copy(r_col[:, :], stat_bank[:, 8:8 + CC])
            dve.tensor_copy(c1[:, :], stat_bank[:, 10:10 + CC]).then_inc(bias_step, 1)
            dve.tensor_copy(s0[:, :], stat_bank[:, 12:13]).then_inc(bias_step, 1)
            dve.tensor_tensor(bias_out[:, :], o_bank[0][:, 0:DIM], bo_row[:, :], ALU.add).then_inc(bias_step, 1)

            attention(0, False, True)
            project(0, True)
            with dve.Fori(1, BATCHES - 1) as b:
                attention(b, True, True)
                project(b, True)
            attention(BATCHES - 1, True, False)
            project(BATCHES - 1, False)
            logits(BATCHES - 1)
            maxima(BATCHES - 1)
            weights(BATCHES - 1)
            split_attn(BATCHES - 1)
            final_sum(BATCHES - 1)

        @block.tensor
        def _(pe):
            def product(dst, pairs):
                passes = [(a, b) for (a_hi, a_lo), (b_hi, b_lo) in pairs
                          for a, b in ((a_hi, b_hi), (a_hi, b_lo), (a_lo, b_hi))]
                for i, (a, b) in enumerate(passes):
                    last = pe.matmul(dst, a, b, start=(i == 0), stop=(i == len(passes) - 1))
                return last

            def transpose_tokens(src):
                for c in range(CC):
                    for t in range(TT):
                        last = pe.transpose(trans_bank[:, c * TOKENS + t * P:c * TOKENS + (t + 1) * P],
                                            src[:, t, c * P:(c + 1) * P], ident[:, :])
                return last

            def group_mean(k, b):
                pe.wait_ge(stat_in[k], 2 * b + 1)
                pe.matmul(stat_bank[:, 0:CC], group_avg[:, :], mv[k][:, :, 0], start=True, stop=True).then_inc(stat_sum[k], 1)

            def group_variance(k, b):
                pe.wait_ge(stat_in[k], 2 * b + 2)
                pe.matmul(stat_bank[:, CC:2 * CC], group_avg[:, :], shift[k][:, 0, :], start=True, stop=True).then_inc(stat_sum[k], 1)

            def project_kv(b, i):
                axis, t = 1 - i // TT, i % TT
                if i == 0:
                    pe.wait_ge(xn_split[0], b + 1)
                    pe.wait_ge(blk_masked, BLOCKS * b)
                if i >= BANKS:
                    pe.wait_ge(kv_lo_done, 4 * b + i - BANKS + 1)
                if i == TT:
                    pe.wait_ge(turned, b + 1)
                hi, lo = (xt_hi, xt_lo) if axis == 0 else (xn_hi[0], xn_lo[0])
                product(ring[i % BANKS][:, :],
                        [((hi[:, c, t * P:(t + 1) * P], lo[:, c, t * P:(t + 1) * P]),
                          (wqkv_hi[:, axis, c, DIM:3 * DIM], wqkv_lo[:, axis, c, DIM:3 * DIM])) for c in range(CC)]
                        ).then_inc(kv_proj, 1)

            def project_q(b, i):
                axis = 1 - i
                hi, lo = (xt_hi, xt_lo) if axis == 0 else (xn_hi[0], xn_lo[0])
                pe.wait_ge(kv_lo_done, 4 * b + 2 + i)
                for m in range(CC):
                    last = product(ring[1 + i][:, m * TOKENS:(m + 1) * TOKENS],
                                   [((wqkv_hi[:, axis, c, m * P:(m + 1) * P], wqkv_lo[:, axis, c, m * P:(m + 1) * P]),
                                     (hi[:, c, :], lo[:, c, :])) for c in range(CC)])
                last.then_inc(q_proj, 1)

            def key_value_block(b, n):
                axis, t, quad = block_of(n)
                rows = slice(QUAD * quad, QUAD * (quad + 1))
                if n == 0:
                    pe.wait_ge(kv_lo_done, 4 * (b + 1))
                elif n < BANKS:
                    pe.wait_ge(q_lo_done, 2 * b + n)
                else:
                    pe.wait_ge(blk_masked, BLOCKS * b + n - BANKS + 1)
                for c in range(CC):
                    chunk = slice(c * P, (c + 1) * P)
                    last = product(ring[n % BANKS][:, c * 2 * P:(c + 1) * 2 * P],
                                   [((k_hi[rows, axis, t, chunk], k_lo[rows, axis, t, chunk]),
                                     (v_hi[rows, axis, t, :, chunk], v_lo[rows, axis, t, :, chunk]))])
                last.then_inc(blk_ready, 1)

            def query_block(b, n):
                axis, t, quad = block_of(n)
                if n == 0:
                    pe.wait_ge(q_lo_done, 2 * (b + 1))
                    pe.wait_ge(t_lo_done, b)
                if n == TT * QUADS:
                    pe.wait_ge(vp_lo_done, b)
                if n in POOL_LO:
                    pe.wait_ge(blk_lo_pool, len(POOL_LO) * b + POOL_LO.index(n) + 1)
                else:
                    pe.wait_ge(blk_lo_dve, len(DVE_LO) * b + DVE_LO.index(n) + 1)
                for c in range(CC):
                    for s in range(2):
                        first = (8 * t + 2 * quad + s) * SIDE
                        seq = slice(first, first + SIDE)
                        last = product(o_bank[axis][:, c * TOKENS + first:c * TOKENS + first + SIDE],
                                       [((kv_hi[:, n % SLOTS, c, s, :], kv_lo[:, n % SLOTS, c, s, :]),
                                         (q_hi[:, axis, c, seq], q_lo[:, axis, c, seq]))])
                last.then_inc(blk_used, 1)

            def scores(b):
                pe.wait_ge(t_lo_done, b + 1)
                pe.wait_ge(x1_ready, b + 1)
                for t in range(TT):
                    last = product(y_bank[:, t * TOKENS:(t + 1) * TOKENS],
                                   [((t_hi[:, c, t * P:(t + 1) * P], t_lo[:, c, t * P:(t + 1) * P]),
                                     (xn_hi[1][:, c, :], xn_lo[1][:, c, :])) for c in range(CC)])
                last.then_inc(s_ready, 1)

            def transpose_weights(b):
                pe.wait_ge(attn_ready, b + 1)
                pe.wait_ge(xn_ready[1], b + 1)
                for j in range(TT):
                    for i in range(TT):
                        last = pe.transpose(trans_bank[:, (j * TT + i) * P:(j * TT + i + 1) * P],
                                            attn[:, i, j * P:(j + 1) * P], ident[:, :])
                last.then_inc(at_ready, 1)

            def weighted_values(b):
                pe.wait_ge(at_lo_done, b + 1)
                pe.wait_ge(vp_lo_done, b + 1)
                pe.wait_ge(logits_done, b + 1)
                for i in range(TT):
                    last = product(y_bank[:, i * DIM:(i + 1) * DIM],
                                   [((at_hi[:, j, i, :], at_lo[:, j, i, :]), (vp_hi[:, j, :], vp_lo[:, j, :])) for j in range(TT)])
                last.then_inc(pv_ready, 1)

            def transpose_x(b):
                pe.wait_ge(x_loaded, 16 * (b + 1))
                transpose_tokens(x_in).then_inc(xt_ready[0], 1)

            def attention(b, has_prev, has_next):
                for n in range(BLOCKS + LAG):
                    if n < BLOCKS:
                        key_value_block(b, n)
                    if n >= LAG:
                        query_block(b, n - LAG)
                    if n == 5 and has_prev:
                        transpose_weights(b - 1)
                    if n == 7 and has_prev:
                        weighted_values(b - 1)
                    if n == 8 and has_next:
                        transpose_x(b + 1)
                    if n == 11 and has_next:
                        group_mean(0, b + 1)
                    if n == 13 and has_next:
                        group_variance(0, b + 1)

            def project(b, has_next):
                pe.wait_ge(o_lo_done, 2 * (b + 1))
                pe.wait_ge(out_ready, b)
                for t in range(TT):
                    last = product(y_bank[:, t * DIM:(t + 1) * DIM],
                                   [((o_hi[:, axis, c, t * P:(t + 1) * P], o_lo[:, axis, c, t * P:(t + 1) * P]),
                                     (wout_hi[:, axis, c, :], wout_lo[:, axis, c, :])) for axis in range(2) for c in range(CC)])
                last.then_inc(y_ready, 1)
                if has_next:
                    project_kv(b + 1, 0)
                    project_kv(b + 1, 1)
                pe.wait_ge(x1_ready, b + 1)
                if has_next:
                    pe.wait_ge(xn_ready[0], b + 2)
                transpose_tokens(x1).then_inc(xt_ready[1], 1)
                if has_next:
                    project_kv(b + 1, 2)
                group_mean(1, b)
                if has_next:
                    project_kv(b + 1, 3)
                group_variance(1, b)
                if has_next:
                    project_q(b + 1, 0)
                    project_q(b + 1, 1)
                pe.wait_ge(xn_split[1], b + 1)
                for m in range(CC):
                    last = product(o_bank[0][:, m * TOKENS:(m + 1) * TOKENS],
                                   [((g_hi[:, c, m * P:(m + 1) * P], g_lo[:, c, m * P:(m + 1) * P]),
                                     (xn_hi[1][:, c, :], xn_lo[1][:, c, :])) for c in range(CC)])
                last.then_inc(t_ready, 1)
                pe.wait_ge(coef_ready[1], b + 1)
                for t in range(TT):
                    for c in range(CC):
                        last = pe.matmul(stat_bank[:, 2 * CC + t:2 * CC + t + 1], xn[1][:, c, t * P:(t + 1) * P],
                                         r_col[:, c:c + 1], start=(c == 0), stop=(c == CC - 1))
                last.then_inc(row_ready, 1)
                for t in range(TT):
                    last = product(o_bank[1][:, t * DIM:(t + 1) * DIM],
                                   [((xn_hi[1][:, c, t * P:(t + 1) * P], xn_lo[1][:, c, t * P:(t + 1) * P]),
                                     (wvo_hi[:, c, :], wvo_lo[:, c, :])) for c in range(CC)])
                last.then_inc(vp_ready, 1)
                scores(b)
                pe.wait_ge(row_done, b + 1)

            pe.wait_ge(consts_ready, 1)
            transpose_x(0)
            group_mean(0, 0)
            group_variance(0, 0)
            pe.wait_ge(w_split, 1)
            project_kv(0, 0)
            project_kv(0, 1)
            pe.wait_ge(w_split, 2)
            project_kv(0, 2)
            project_kv(0, 3)
            project_q(0, 0)
            project_q(0, 1)

            pe.wait_ge(l1_loaded, 4 * 16)
            pe.wait_ge(xn_ready[0], 1)
            for e in range(CC):
                for o in range(CC):
                    last = pe.transpose(trans_bank[:, e * DIM + o * P:e * DIM + (o + 1) * P], wl1[:, 3, o, e * P:(e + 1) * P], ident[:, :])
            last.then_inc(wot_ready, 1)
            for m in range(CC):
                for e in range(CC):
                    last = pe.matmul(y_bank[:, m * DIM:(m + 1) * DIM], wl1[:, 0, e, m * P:(m + 1) * P], wl1[:, 1, e, :],
                                     start=(e == 0), stop=(e == CC - 1))
            last.then_inc(fold_ready, 1)
            pe.wait_ge(wot_done, 1)
            for m in range(CC):
                for e in range(CC):
                    last = pe.matmul(o_bank[1][:, m * DIM:(m + 1) * DIM], wl1[:, 2, e, m * P:(m + 1) * P], wo_t[:, e, :],
                                     start=(e == 0), stop=(e == CC - 1))
            last.then_inc(fold_ready, 1)
            pe.wait_ge(bias_step, 2)
            for i, (weight, vector) in enumerate(((0, 1), (1, 0))):
                for m in range(CC):
                    for e in range(CC):
                        pe.matmul(stat_bank[:, 8 + 2 * i + m:9 + 2 * i + m], wl1[:, weight, e, m * P:(m + 1) * P],
                                  bias_in[:, vector, e:e + 1], start=(e == 0), stop=(e == CC - 1))
            for e in range(CC):
                pe.matmul(stat_bank[:, 12:13], bq_rep[:, e, :], bias_in[:, 1, e:e + 1], start=(e == 0), stop=(e == CC - 1))
            for e in range(CC):
                last = pe.matmul(o_bank[0][:, 0:DIM], bv2_rep[:, e, :], wo_t[:, e, :], start=(e == 0), stop=(e == CC - 1))
            last.then_inc(fold_ready, 1)
            pe.wait_ge(w_split, 3)
            pe.wait_ge(fold_split, 2)
            pe.wait_ge(bias_step, 5)

            attention(0, False, True)
            project(0, True)
            with pe.Fori(1, BATCHES - 1) as b:
                attention(b, True, True)
                project(b, True)
            attention(BATCHES - 1, True, False)
            project(BATCHES - 1, False)
            transpose_weights(BATCHES - 1)
            weighted_values(BATCHES - 1)


_INS = ['x', 'L0_conv_w_qkv0', 'L0_conv_w_out0', 'L0_conv_w_qkv1', 'L0_conv_w_out1', 'L1_conv_Wq', 'L1_conv_bq',
        'L1_conv_Wk', 'L1_conv_bk', 'L1_conv_Wv', 'L1_conv_bv', 'L1_conv_Wo', 'L1_conv_bo', 'L1_conv_sigma']
_OUTS = [((8, 16, 16, 256), 'float32')]


def kernel(**inputs):
    import numpy as _np
    import concourse.bacc as _bacc
    from concourse import mybir as _mybir
    from concourse.bass_utils import run_bass_kernel_spmd as _run

    nc = _bacc.Bacc("TRN2", target_bir_lowering=False, num_devices=1)
    arrays, args = {}, []
    for name in _INS:
        a = _np.ascontiguousarray(inputs[name])
        arrays[f"in_{name}_dram"] = a
        args.append(nc.dram_tensor(f"in_{name}_dram", a.shape, _mybir.dt.from_np(a.dtype), kind="ExternalInput").ap())
    for i, (shape, dtype) in enumerate(_OUTS):
        dt = _mybir.dt.from_np(_np.dtype(dtype))
        args.append(nc.dram_tensor(f"out_{i}_dram", shape, dt, kind="ExternalOutput").ap())
    build(nc, *args)
    r = _run(nc, [arrays], core_ids=[0])
    return r.results[0]["out_0_dram"]
```

```python
import concourse.bass as bass
from concourse import mybir
from contextlib import ExitStack

FP32 = mybir.dt.float32
FP32R = mybir.dt.float32r
INT32 = mybir.dt.int32
ALU = mybir.AluOpType
ACT = mybir.ActivationFunctionType
AX = mybir.AxisListType

BATCHES, SIDE, DIM = 8, 16, 256
TOKENS = SIDE * SIDE
P = 128
TT = TOKENS // P
CC = DIM // P
HEAD = 16
GROUP = 8
EPS = 1e-5
QUAD = 32
QUADS = P // QUAD
TILES = 2 * TT
PAIR = 32
PAIRS = P // PAIR
FAR = 1.0e30


def tile_of(n):
    return n // TT, n % TT


def build(nc, x, w_qkv0, w_out0, w_qkv1, w_out1, wq, bq, wk, bk, wv, bv, wo, bo, sigma, out):
    with ExitStack() as ctx:
        def sb(name, shape, dt=FP32):
            return ctx.enter_context(nc.sbuf_tensor(name, shape, dt))

        def sem(name):
            return ctx.enter_context(nc.semaphore(name))

        wqkv_in = sb("wqkv_in", [P, 2, CC, 3 * DIM])
        wqkv_hi = sb("wqkv_hi", [P, 2, CC, 3 * DIM], FP32R)
        wqkv_lo = sb("wqkv_lo", [P, 2, CC, 3 * DIM], FP32R)
        wout_in = sb("wout_in", [P, 2, CC, DIM])
        wout_hi = sb("wout_hi", [P, 2, CC, DIM], FP32R)
        wout_lo = sb("wout_lo", [P, 2, CC, DIM], FP32R)
        wl1 = sb("wl1", [P, 4, CC, DIM])
        wo_t = sb("wo_t", [P, CC, DIM])
        g_hi = sb("g_hi", [P, CC, DIM], FP32R)
        g_lo = sb("g_lo", [P, CC, DIM], FP32R)
        wvo_hi = sb("wvo_hi", [P, CC, DIM], FP32R)
        wvo_lo = sb("wvo_lo", [P, CC, DIM], FP32R)
        bias_in = sb("bias_in", [P, 3, CC])
        bq_rep = sb("bq_rep", [P, CC, P])
        bv2_rep = sb("bv2_rep", [P, CC, P])
        bo_row = sb("bo_row", [P, DIM])
        bias_out = sb("bias_out", [P, DIM])
        c1 = sb("c1", [P, CC])
        r_col = sb("r_col", [P, CC])
        s0 = sb("s0", [P, 1])
        sig = sb("sig", [P, 1])
        neg_gw = sb("neg_gw", [P, 1])
        iota_row = sb("iota_row", [P, 1], INT32)
        iota_j = sb("iota_j", [P, 4, TOKENS], INT32)
        ji = sb("ji", [P, 4, TOKENS])
        part_i = sb("part_i", [P, 4], INT32)
        pi = sb("pi", [P, 4])
        par_i = sb("par_i", [P, 1], INT32)
        par_f = sb("par_f", [P, 1])
        parity = sb("parity", [P, 2])
        ident = sb("ident", [P, P])
        group_avg = sb("group_avg", [P, P])
        head_mask = sb("head_mask", [P, 2 * CC * 2, PAIR])
        row_mask = sb("row_mask", [P, P])
        col_mask = sb("col_mask", [P, TT, TOKENS])
        hcol = sb("hcol", [P, TT])
        scratch = sb("scratch", [P, 2, TOKENS])
        gate = sb("gate", [P, 1])
        minus_half = sb("minus_half", [P, CC])
        x_in = sb("x_in", [P, TT, DIM])
        x_res = sb("x_res", [P, TT, DIM])
        moments = [sb(f"moments{k}", [P, CC, 6]) for k in range(2)]
        mv = [sb(f"mv{k}", [P, CC, 2]) for k in range(2)]
        gmean = [sb(f"gmean{k}", [P, CC]) for k in range(2)]
        shift = [sb(f"shift{k}", [P, 2, CC]) for k in range(2)]
        var_eps = [sb(f"var_eps{k}", [P, CC]) for k in range(2)]
        rstd = [sb(f"rstd{k}", [P, CC]) for k in range(2)]
        nbias = [sb(f"nbias{k}", [P, CC]) for k in range(2)]
        xn = [sb(f"xn{k}", [P, CC, TOKENS]) for k in range(2)]
        xn_hi = [sb(f"xn_hi{k}", [P, CC, TOKENS], FP32R) for k in range(2)]
        xn_lo = [sb(f"xn_lo{k}", [P, CC, TOKENS], FP32R) for k in range(2)]
        xt_hi = sb("xt_hi", [P, CC, TOKENS], FP32R)
        xt_lo = sb("xt_lo", [P, CC, TOKENS], FP32R)
        k = sb("k", [P, 2, TT, DIM])
        v = sb("v", [P, 2, TT, 2, DIM])
        q = sb("q", [P, 2, CC, TOKENS])
        kv = sb("kv", [P, 2, QUADS, CC, 2, PAIR])
        o_even = sb("o_even", [P, CC, PAIRS, PAIR])
        o_tok = sb("o_tok", [P, 2, TT, DIM])
        o_hi = sb("o_hi", [P, 2, CC, TOKENS], FP32R)
        o_lo = sb("o_lo", [P, 2, CC, TOKENS], FP32R)
        x1 = sb("x1", [P, TT, DIM])
        x1b = sb("x1b", [P, TT, DIM])
        t_hi = sb("t_hi", [P, CC, TOKENS], FP32R)
        t_lo = sb("t_lo", [P, CC, TOKENS], FP32R)
        vp_hi = sb("vp_hi", [P, TT, DIM], FP32R)
        vp_lo = sb("vp_lo", [P, TT, DIM], FP32R)
        row_term = sb("row_term", [P, TT])
        log_row = sb("log_row", [P, TT, P])
        log_col = sb("log_col", [P, TT, TOKENS])
        neg_max = sb("neg_max", [P, 2, TT])
        exp_row = sb("exp_row", [P, TT, P])
        exp_col = sb("exp_col", [P, TT, TOKENS])
        exp_sum = sb("exp_sum", [P, 2, TT])
        inv_sum = sb("inv_sum", [P, 2, TT])
        attn = sb("attn", [P, TT, TOKENS])
        at_hi = sb("at_hi", [P, TT, TT, P], FP32R)
        at_lo = sb("at_lo", [P, TT, TT, P], FP32R)
        y_out = sb("y_out", [P, TT, DIM])
        bank = [ctx.enter_context(nc.psum_tensor(f"bank{i}", [P, 512], FP32)) for i in range(8)]
        trans_bank, stat_bank = bank[0], bank[1]
        kv_bank = [bank[2:4], bank[4:6]]
        qkv_bank = bank[6:8]
        ot_bank = bank[2:4]
        y_bank, proj_bank, q_bank = bank[4], [bank[5], bank[6], bank[7], bank[2]], [bank[3], bank[5]]
        t_bank, vp_bank, s_bank, pv_bank = bank[6], bank[7], bank[4], bank[0]

        x_loaded, stored = sem("x_loaded"), sem("stored")
        w_loaded = [sem(f"w_loaded{i}") for i in range(2)]
        wout_loaded, l1_loaded, bias_loaded = sem("wout_loaded"), sem("l1_loaded"), sem("bias_loaded")
        iota_done, const_step, consts_ready = sem("iota_done"), sem("const_step"), sem("consts_ready")
        w_hi_done, w_split = sem("w_hi_done"), sem("w_split")
        fold_ready, fold_hi_done, fold_split = sem("fold_ready"), sem("fold_hi_done"), sem("fold_split")
        wot_ready, wot_done, bias_step = sem("wot_ready"), sem("wot_done"), sem("bias_step")
        xt_ready = [sem(f"xt_ready{k}") for k in range(2)]
        norm_step = [sem(f"norm_step{k}") for k in range(2)]
        stat_in = [sem(f"stat_in{k}") for k in range(2)]
        stat_sum = [sem(f"stat_sum{k}") for k in range(2)]
        var_ready = [sem(f"var_ready{k}") for k in range(2)]
        rstd_ready = [sem(f"rstd_ready{k}") for k in range(2)]
        coef_ready = [sem(f"coef_ready{k}") for k in range(2)]
        xn_ready = [sem(f"xn_ready{k}") for k in range(2)]
        xn_hi_done = [sem(f"xn_hi_done{k}") for k in range(2)]
        xn_split = [sem(f"xn_split{k}") for k in range(2)]
        res_ready, turned = sem("res_ready"), sem("turned")
        kv_proj, kv_act, kv_dve = sem("kv_proj"), sem("kv_act"), sem("kv_dve")
        q_proj, q_act, q_dve = sem("q_proj"), sem("q_act"), sem("q_dve")
        pair_done, pe_waited = sem("pair_done"), sem("pe_waited")
        kv_ready, kv_masked, o_ready = sem("kv_ready"), sem("kv_masked"), sem("o_ready")
        o_even_done, o_done, ot_ready = sem("o_even_done"), sem("o_done"), sem("ot_ready")
        o_hi_done, o_lo_done = sem("o_hi_done"), sem("o_lo_done")
        y_ready, x1_ready, x1b_ready = sem("y_ready"), sem("x1_ready"), sem("x1b_ready")
        t_ready, t_hi_done, t_lo_done = sem("t_ready"), sem("t_hi_done"), sem("t_lo_done")
        row_ready, row_done = sem("row_ready"), sem("row_done")
        vp_ready, vp_hi_done, vp_lo_done = sem("vp_ready"), sem("vp_hi_done"), sem("vp_lo_done")
        s_ready, logits_done, max_ready = sem("s_ready"), sem("logits_done"), sem("max_ready")
        exp_done, soft_step, attn_ready = sem("exp_done"), sem("soft_step"), sem("attn_ready")
        at_ready, at_hi_done, at_lo_done = sem("at_ready"), sem("at_hi_done"), sem("at_lo_done")
        pv_ready, out_ready = sem("pv_ready"), sem("out_ready")

        x_dram = x.rearrange("b h w d -> b (h w) d")
        out_dram = out.rearrange("b h w d -> b (h w) d")

        def by_axis(ap, axis):
            return ap.rearrange("p (h w) -> p w h", h=SIDE) if axis == 0 else ap.rearrange("p (h w) -> p h w", h=SIDE)

        block = ctx.enter_context(nc.Block())

        @block.sync
        def _(sp):
            def load_x(b):
                sp.dma_start(x_in[:, :, :], x_dram[bass.ds(b, 1), :, :].rearrange("a (t p) d -> p (a t) d", p=P)
                             ).then_inc(x_loaded, 16)

            def store_y(b):
                sp.wait_ge(out_ready, b + 1)
                sp.dma_start(out_dram[bass.ds(b, 1), :, :].rearrange("a (t p) d -> p (a t) d", p=P), y_out[:, :, :]
                             ).then_inc(stored, 16)

            load_x(0)
            sp.dma_start(wqkv_in[:, 1, :, :], w_qkv1.rearrange("(c p) n -> p c n", p=P)).then_inc(w_loaded[1], 16)
            sp.dma_start(wout_in[:, 0, :, :], w_out0.rearrange("(c p) n -> p c n", p=P)).then_inc(wout_loaded, 16)
            for i, w in enumerate((wq, wk)):
                sp.dma_start(wl1[:, i, :, :], w.rearrange("(c p) n -> p c n", p=P)).then_inc(l1_loaded, 16)

            def batch(b, has_prev, has_next):
                if has_next:
                    sp.wait_ge(xt_ready[0], b + 1)
                    sp.wait_ge(res_ready, b + 1)
                    load_x(b + 1)
                if has_prev:
                    store_y(b - 1)

            batch(0, False, True)
            with sp.Fori(1, BATCHES - 1) as b:
                batch(b, True, True)
            batch(BATCHES - 1, True, False)
            store_y(BATCHES - 1)
            sp.wait_ge(stored, 16 * BATCHES)

        @block.gpsimd
        def _(pool):
            pool.iota(iota_row[:, :], [[0, 1]], base=0, channel_multiplier=1).then_inc(iota_done, 1)
            for i, pattern in enumerate(([[1, 256]], [[1, 16], [0, 16]], [[0, 16], [1, 16]], [[1, 32], [0, 8]])):
                pool.iota(iota_j[:, i, :], pattern, base=0, channel_multiplier=0).then_inc(iota_done, 1)

            def turn(b):
                if not (isinstance(b, int) and b == 0):
                    pool.wait_ge(q_proj, 2 * b)
                pool.wait_ge(xn_hi_done[0], b + 1)
                for c in range(CC):
                    pool.tensor_tensor(xt_lo[:, c, :].rearrange("p (w h) -> p w h", w=SIDE), by_axis(xn[0][:, c, :], 0),
                                       by_axis(xn_hi[0][:, c, :].bitcast(FP32), 0), ALU.subtract)
                for c in range(CC):
                    last = pool.tensor_copy(xt_hi[:, c, :].rearrange("p (w h) -> p w h", w=SIDE), by_axis(xn_hi[0][:, c, :], 0))
                last.then_inc(turned, 1)

            def inverse_root(k, b):
                pool.wait_ge(var_ready[k], b + 1)
                pool.tensor_tensor(rstd[k][:, :], var_eps[k][:, :], minus_half[:, :], ALU.pow).then_inc(rstd_ready[k], 1)

            pool.memset(minus_half[:, :], -0.5).then_inc(iota_done, 1)
            pool.wait_ge(iota_done, 6)
            inverse_root(0, 0)
            turn(0)

            def batch(b, has_next):
                if has_next:
                    inverse_root(0, b + 1)
                    turn(b + 1)
                pool.wait_ge(x1_ready, b + 1)
                pool.wait_ge(out_ready, b)
                for t in range(TT):
                    last = pool.tensor_tensor(x1b[:, t, :], x1[:, t, :], bias_out[:, :], ALU.add)
                last.then_inc(x1b_ready, 1)
                inverse_root(1, b)

            pool.wait_ge(bias_step, 5)
            batch(0, True)
            with pool.Fori(1, BATCHES - 1) as b:
                batch(b, True)
            batch(BATCHES - 1, False)

        @block.scalar
        def _(act):
            act.dma_start(sig[:, :], sigma.rearrange("(a n) -> a n", a=1).partition_broadcast(P)).then_inc(bias_loaded, 16)
            act.dma_start(wqkv_in[:, 0, :, :], w_qkv0.rearrange("(c p) n -> p c n", p=P)).then_inc(w_loaded[0], 16)
            act.dma_start(wout_in[:, 1, :, :], w_out1.rearrange("(c p) n -> p c n", p=P)).then_inc(wout_loaded, 16)
            for i, w in ((2, wv), (3, wo)):
                act.dma_start(wl1[:, i, :, :], w.rearrange("(c p) n -> p c n", p=P)).then_inc(l1_loaded, 16)
            for i, vector in enumerate((bq, bk, bv)):
                act.dma_start(bias_in[:, i, :], vector.rearrange("(c p) -> p c", p=P), allow_slow_non_contiguous=True).then_inc(bias_loaded, 16)
            act.dma_start(bo_row[:, :], bo.rearrange("(a n) -> a n", a=1).partition_broadcast(P)).then_inc(bias_loaded, 16)

            def copy_residual(b):
                act.wait_ge(x_loaded, 16 * (b + 1))
                act.wait_ge(x1_ready, b)
                act.activation(x_res[:, :, :], x_in[:, :, :], ACT.Copy).then_inc(res_ready, 1)

            def normalise(k, b):
                act.wait_ge(coef_ready[k], b + 1)
                act.wait_ge(xn_split[k], b)
                if k == 0:
                    act.wait_ge(turned, b)
                for c in range(CC):
                    last = act.activation(xn[k][:, c, :], trans_bank[:, c * TOKENS:(c + 1) * TOKENS], ACT.Identity,
                                          bias=nbias[k][:, c:c + 1], scale=rstd[k][:, c:c + 1])
                last.then_inc(xn_ready[k], 1)

            def take_kv(b, i):
                axis, t = 1 - i // TT, i % TT
                src = proj_bank[i]
                act.wait_ge(kv_proj, TILES * b + i + 1)
                act.activation(k[:, axis, t, :], src[:, 0:DIM], ACT.Copy)
                for s in range(2):
                    last = act.activation(v[:, axis, t, s, :], src[:, DIM:2 * DIM], ACT.Copy, scale=parity[:, s:s + 1])
                last.then_inc(kv_act, 1)

            def take_q(b):
                act.wait_ge(q_proj, 2 * b + 1)
                act.activation(q[:, 1, :, :].rearrange("p c n -> p (c n)"), q_bank[0][:, :], ACT.Copy).then_inc(q_act, 1)

            def take_even(b, n):
                act.wait_ge(o_ready, TILES * b + n + 1)
                for r in range(2):
                    last = act.activation(o_even[:, :, 2 * r:2 * r + 2, :].rearrange("p c a e -> p c (a e)"),
                                          qkv_bank[r][:, 0:P].rearrange("p (c a) -> p c a", c=CC), ACT.Copy, scale=parity[:, 0:1])
                last.then_inc(o_even_done, 1)

            def split_o(b, axis):
                act.wait_ge(ot_ready, 2 * b + axis + 1)
                for c in range(CC):
                    last = act.activation(by_axis(o_hi[:, axis, c, :], axis),
                                          ot_bank[axis][:, c * TOKENS:(c + 1) * TOKENS].rearrange("p (s i) -> p s i", s=SIDE), ACT.Copy)
                last.then_inc(o_hi_done, 1)

            def exponentials(b):
                act.wait_ge(max_ready, b + 1)
                for t in range(TT):
                    act.activation(exp_row[:, t, :], log_row[:, t, :], ACT.Exp, bias=neg_max[:, 0, t:t + 1],
                                   accum_out=exp_sum[:, 0, t:t + 1])
                    last = act.activation(exp_col[:, t, :], log_col[:, t, :], ACT.Exp, bias=neg_max[:, 1, t:t + 1],
                                          accum_out=exp_sum[:, 1, t:t + 1])
                last.then_inc(exp_done, 1)

            def split_attn(b):
                act.wait_ge(at_ready, b + 1)
                act.activation(at_hi[:, :, :, :].rearrange("p j i q -> p (j i q)"), trans_bank[:, :], ACT.Copy).then_inc(at_hi_done, 1)

            def attention(b, has_prev, has_next):
                if has_prev:
                    exponentials(b - 1)
                take_even(b, 0)
                if has_prev:
                    split_attn(b - 1)
                take_even(b, 1)
                take_even(b, 2)
                split_o(b, 0)
                if has_next:
                    normalise(0, b + 1)
                take_even(b, 3)
                split_o(b, 1)

            def project(b, has_next):
                if has_next:
                    take_kv(b + 1, 0)
                    copy_residual(b + 1)
                    take_kv(b + 1, 2)
                    take_q(b + 1)
                normalise(1, b)
                act.wait_ge(t_ready, b + 1)
                for c in range(CC):
                    last = act.activation(t_hi[:, c, :], t_bank[:, c * TOKENS:(c + 1) * TOKENS], ACT.Identity, bias=c1[:, c:c + 1])
                last.then_inc(t_hi_done, 1)
                act.wait_ge(vp_ready, b + 1)
                act.activation(vp_hi[:, :, :].rearrange("p t d -> p (t d)"), vp_bank[:, :], ACT.Copy).then_inc(vp_hi_done, 1)

            copy_residual(0)
            act.wait_ge(consts_ready, 1)
            for axis in (1, 0):
                act.wait_ge(w_loaded[axis], 16)
                act.activation(wqkv_hi[:, axis, :, 0:DIM], wqkv_in[:, axis, :, 0:DIM], ACT.Copy, scale=DIM ** -0.5)
                act.activation(wqkv_hi[:, axis, :, DIM:3 * DIM], wqkv_in[:, axis, :, DIM:3 * DIM], ACT.Copy).then_inc(w_hi_done, 1)
                if axis == 1:
                    normalise(0, 0)
            act.wait_ge(wout_loaded, 32)
            act.activation(wout_hi[:, :, :, :].rearrange("p a c n -> p (a c n)"),
                           wout_in[:, :, :, :].rearrange("p a c n -> p (a c n)"), ACT.Copy).then_inc(w_hi_done, 1)
            take_kv(0, 0)
            take_kv(0, 2)
            take_q(0)
            for i, (dst, src) in enumerate(((g_hi, y_bank), (wvo_hi, vp_bank))):
                act.wait_ge(fold_ready, i + 1)
                act.activation(dst[:, :, :].rearrange("p c n -> p (c n)"), src[:, :], ACT.Copy).then_inc(fold_hi_done, 1)

            attention(0, False, True)
            project(0, True)
            with act.Fori(1, BATCHES - 1) as b:
                attention(b, True, True)
                project(b, True)
            attention(BATCHES - 1, True, False)
            project(BATCHES - 1, False)
            exponentials(BATCHES - 1)
            split_attn(BATCHES - 1)

        @block.vector
        def _(dve):
            steps = [0]

            def const(inst):
                inst.then_inc(const_step, 1)
                steps[0] += 1
                dve.wait_ge(const_step, steps[0])

            dve.wait_ge(iota_done, 5)
            const(dve.tensor_copy(ji[:, :, :], iota_j[:, :, :]))
            for i, (shift_by, keep) in enumerate(((0, 0x7f), (4, 0x7f), (0, 15), (3, 0x7f))):
                dve.tensor_scalar(part_i[:, i:i + 1], iota_row[:, :], shift_by, keep, ALU.logical_shift_right, ALU.bitwise_and)
            const(dve.tensor_scalar(par_i[:, :], iota_row[:, :], 4, 1, ALU.logical_shift_right, ALU.bitwise_and))
            dve.tensor_copy(par_f[:, :], par_i[:, :])
            const(dve.tensor_copy(pi[:, :], part_i[:, :]))
            dve.tensor_scalar(ident[:, :], ji[:, 0, 0:P], pi[:, 0:1], None, ALU.is_equal)
            dve.tensor_scalar(group_avg[:, :], ji[:, 3, 0:P], pi[:, 3:4], 1.0 / GROUP, ALU.is_equal, ALU.mult)
            for i in range(2 * CC * 2):
                dve.tensor_scalar(head_mask[:, i, :], ji[:, 1, 0:PAIR], par_f[:, :], None, ALU.is_equal)
            const(dve.tensor_copy(parity[:, 1:2], par_i[:, :]))
            dve.tensor_scalar(parity[:, 0:1], parity[:, 1:2], -1.0, 1.0, ALU.mult, ALU.add).then_inc(consts_ready, 1)

            def statistics(k, b):
                dve.wait_ge(xt_ready[k], b + 1)
                for c in range(CC):
                    last = dve.bn_stats(moments[k][:, c, :], trans_bank[:, c * TOKENS:(c + 1) * TOKENS])
                last.then_inc(norm_step[k], 1)
                dve.wait_ge(norm_step[k], 4 * b + 1)
                dve.memset(gate[:, :], 0.0)
                for c in range(CC):
                    last = dve.bn_aggr(mv[k][:, c, :], moments[k][:, c, :])
                last.then_inc(stat_in[k], 1)

            def spread(k, b):
                dve.wait_ge(stat_sum[k], 2 * b + 1)
                dve.tensor_copy(gmean[k][:, :], stat_bank[:, 0:CC]).then_inc(norm_step[k], 1)
                dve.wait_ge(norm_step[k], 4 * b + 2)
                dve.tensor_tensor(shift[k][:, 0, :], mv[k][:, :, 0], gmean[k][:, :], ALU.subtract).then_inc(norm_step[k], 1)
                dve.wait_ge(norm_step[k], 4 * b + 3)
                dve.tensor_tensor(shift[k][:, 1, :], shift[k][:, 0, :], shift[k][:, 0, :], ALU.mult).then_inc(norm_step[k], 1)
                dve.wait_ge(norm_step[k], 4 * b + 4)
                dve.tensor_tensor(shift[k][:, 0, :], shift[k][:, 1, :], mv[k][:, :, 1], ALU.add).then_inc(stat_in[k], 1)

            def variance(k, b):
                dve.wait_ge(stat_sum[k], 2 * b + 2)
                dve.tensor_scalar(var_eps[k][:, :], stat_bank[:, CC:2 * CC], EPS, None, ALU.add).then_inc(var_ready[k], 1)

            def coefficients(k, b):
                dve.wait_ge(rstd_ready[k], b + 1)
                dve.scalar_tensor_tensor(nbias[k][:, :], gmean[k][:, :], -1.0, rstd[k][:, :], ALU.mult, ALU.mult).then_inc(coef_ready[k], 1)

            def split_xn(k, b):
                dve.wait_ge(xn_ready[k], b + 1)
                dve.tensor_copy(xn_hi[k][:, :, :], xn[k][:, :, :]).then_inc(xn_hi_done[k], 1)
                dve.wait_ge(xn_hi_done[k], b + 1)
                dve.tensor_tensor(xn_lo[k][:, :, :], xn[k][:, :, :], xn_hi[k][:, :, :].bitcast(FP32), ALU.subtract).then_inc(xn_split[k], 1)

            def take_kv(b, i):
                axis, t = 1 - i // TT, i % TT
                src = proj_bank[i]
                dve.wait_ge(kv_proj, TILES * b + i + 1)
                dve.tensor_copy(k[:, axis, t, :], src[:, 0:DIM])
                for s in range(2):
                    last = dve.tensor_scalar(v[:, axis, t, s, :], src[:, DIM:2 * DIM], parity[:, s:s + 1], None, ALU.mult)
                last.then_inc(kv_dve, 1)

            def take_q(b):
                dve.wait_ge(q_proj, 2 * b + 2)
                dve.tensor_copy(q[:, 0, :, :].rearrange("p c n -> p (c n)"), q_bank[1][:, :]).then_inc(q_dve, 1)

            def mask_kv(b, n):
                for r in range(2):
                    dve.wait_ge(kv_ready, (QUADS * TILES) * b + QUADS * n + 3 + r)
                    last = dve.tensor_tensor(kv[:, n % 2, r * 2:r * 2 + 2, :, :, :].rearrange("p a c s e -> p (a c s e)"),
                                             kv_bank[n % 2][r][:, 0:2 * P], head_mask[:, :, :].rearrange("p a e -> p (a e)"), ALU.mult)
                last.then_inc(kv_masked, 1)

            def take_odd(b, n):
                axis, t = tile_of(n)
                dve.wait_ge(o_even_done, TILES * b + n + 1)
                for r in range(2):
                    last = dve.scalar_tensor_tensor(
                        o_tok[:, axis, t, :].rearrange("p (c a) -> p c a", c=CC)[:, :, 2 * r * PAIR:2 * (r + 1) * PAIR],
                        qkv_bank[r][:, P:2 * P].rearrange("p (c a) -> p c a", c=CC), parity[:, 1:2],
                        o_even[:, :, 2 * r:2 * r + 2, :].rearrange("p c a e -> p c (a e)"), ALU.mult, ALU.add)
                last.then_inc(o_done, 1)

            def split_o(b, axis):
                dve.wait_ge(o_hi_done, 2 * b + axis + 1)
                for c in range(CC):
                    last = dve.tensor_tensor(by_axis(o_lo[:, axis, c, :], axis),
                                             ot_bank[axis][:, c * TOKENS:(c + 1) * TOKENS].rearrange("p (s i) -> p s i", s=SIDE),
                                             by_axis(o_hi[:, axis, c, :].bitcast(FP32), axis), ALU.subtract)
                last.then_inc(o_lo_done, 1)

            def logits(b):
                dve.wait_ge(row_done, b + 1)
                dve.wait_ge(s_ready, b + 1)
                for t in range(TT):
                    dve.scalar_tensor_tensor(log_row[:, t, :], s_bank[:, t * TOKENS + t * P:t * TOKENS + (t + 1) * P],
                                             row_term[:, t:t + 1], row_mask[:, :], ALU.add, ALU.add)
                    last = dve.scalar_tensor_tensor(log_col[:, t, :], s_bank[:, t * TOKENS:(t + 1) * TOKENS],
                                                    row_term[:, t:t + 1], col_mask[:, t, :], ALU.add, ALU.add)
                last.then_inc(logits_done, 1)

            def maxima(b):
                dve.wait_ge(logits_done, b + 1)
                dve.tensor_reduce(neg_max[:, 0, :], log_row[:, :, :], AX.X, ALU.max, negate=True)
                dve.tensor_reduce(neg_max[:, 1, :], log_col[:, :, :], AX.X, ALU.max, negate=True).then_inc(max_ready, 1)

            def weights(b):
                dve.wait_ge(exp_done, b + 1)
                dve.reciprocal(inv_sum[:, :, :], exp_sum[:, :, :]).then_inc(soft_step, 1)
                dve.wait_ge(soft_step, 2 * b + 1)
                for t in range(TT):
                    last = dve.tensor_scalar(attn[:, t, :], exp_col[:, t, :], inv_sum[:, 1, t:t + 1], None, ALU.mult)
                last.then_inc(soft_step, 1)
                dve.wait_ge(soft_step, 2 * b + 2)
                for t in range(TT):
                    own = attn[:, t, t * P:(t + 1) * P]
                    last = dve.scalar_tensor_tensor(own, exp_row[:, t, :], inv_sum[:, 0, t:t + 1], own, ALU.mult, ALU.add)
                last.then_inc(attn_ready, 1)

            def split_attn(b):
                dve.wait_ge(at_hi_done, b + 1)
                dve.tensor_tensor(at_lo[:, :, :, :].rearrange("p j i q -> p (j i q)"), trans_bank[:, :],
                                  at_hi[:, :, :, :].rearrange("p j i q -> p (j i q)").bitcast(FP32), ALU.subtract).then_inc(at_lo_done, 1)

            def final_sum(b):
                dve.wait_ge(pv_ready, b + 1)
                dve.wait_ge(x1b_ready, b + 1)
                dve.wait_ge(stored, 16 * b)
                dve.tensor_tensor(y_out[:, :, :].rearrange("p t d -> p (t d)"), pv_bank[:, :],
                                  x1b[:, :, :].rearrange("p t d -> p (t d)"), ALU.add).then_inc(out_ready, 1)

            def attention(b, has_prev, has_next):
                if has_prev:
                    logits(b - 1)
                    maxima(b - 1)
                mask_kv(b, 0)
                if has_prev:
                    weights(b - 1)
                mask_kv(b, 1)
                take_odd(b, 0)
                if has_prev:
                    split_attn(b - 1)
                mask_kv(b, 2)
                if has_prev:
                    final_sum(b - 1)
                take_odd(b, 1)
                if has_next:
                    statistics(0, b + 1)
                mask_kv(b, 3)
                if has_next:
                    spread(0, b + 1)
                take_odd(b, 2)
                if has_next:
                    variance(0, b + 1)
                split_o(b, 0)
                if has_next:
                    coefficients(0, b + 1)
                    split_xn(0, b + 1)
                take_odd(b, 3)
                split_o(b, 1)

            def project(b, has_next):
                dve.wait_ge(y_ready, b + 1)
                dve.wait_ge(res_ready, b + 1)
                dve.wait_ge(x1b_ready, b)
                dve.tensor_tensor(x1[:, :, :].rearrange("p t d -> p (t d)"), y_bank[:, :],
                                  x_res[:, :, :].rearrange("p t d -> p (t d)"), ALU.add).then_inc(x1_ready, 1)
                if has_next:
                    take_kv(b + 1, 1)
                statistics(1, b)
                spread(1, b)
                if has_next:
                    take_kv(b + 1, 3)
                variance(1, b)
                coefficients(1, b)
                split_xn(1, b)
                if has_next:
                    take_q(b + 1)
                dve.wait_ge(t_hi_done, b + 1)
                for c in range(CC):
                    last = dve.scalar_tensor_tensor(t_lo[:, c, :], t_bank[:, c * TOKENS:(c + 1) * TOKENS], c1[:, c:c + 1],
                                                    t_hi[:, c, :].bitcast(FP32), ALU.add, ALU.subtract)
                last.then_inc(t_lo_done, 1)
                dve.wait_ge(row_ready, b + 1)
                dve.tensor_scalar(row_term[:, :], stat_bank[:, 2 * CC:2 * CC + TT], s0[:, :], None, ALU.add).then_inc(row_done, 1)
                dve.wait_ge(vp_hi_done, b + 1)
                dve.tensor_tensor(vp_lo[:, :, :].rearrange("p t d -> p (t d)"), vp_bank[:, :],
                                  vp_hi[:, :, :].rearrange("p t d -> p (t d)").bitcast(FP32), ALU.subtract).then_inc(vp_lo_done, 1)

            statistics(0, 0)
            spread(0, 0)
            variance(0, 0)
            coefficients(0, 0)
            split_xn(0, 0)

            def low_qkv(axis):
                dve.wait_ge(w_hi_done, 2 - axis)
                dve.scalar_tensor_tensor(wqkv_lo[:, axis, :, 0:DIM], wqkv_in[:, axis, :, 0:DIM], DIM ** -0.5,
                                         wqkv_hi[:, axis, :, 0:DIM].bitcast(FP32), ALU.mult, ALU.subtract)
                dve.tensor_tensor(wqkv_lo[:, axis, :, DIM:3 * DIM], wqkv_in[:, axis, :, DIM:3 * DIM],
                                  wqkv_hi[:, axis, :, DIM:3 * DIM].bitcast(FP32), ALU.subtract).then_inc(w_split, 1)

            low_qkv(1)
            low_qkv(0)
            dve.wait_ge(w_hi_done, 3)
            dve.tensor_tensor(wout_lo[:, :, :, :].rearrange("p a c n -> p (a c n)"), wout_in[:, :, :, :].rearrange("p a c n -> p (a c n)"),
                              wout_hi[:, :, :, :].rearrange("p a c n -> p (a c n)").bitcast(FP32), ALU.subtract).then_inc(w_split, 1)
            dve.wait_ge(bias_loaded, 5 * 16)
            dve.memset(scratch[:, 0, 0:P], 1.0).then_inc(bias_step, 1)
            dve.wait_ge(bias_step, 1)
            for c in range(CC):
                dve.tensor_scalar(bq_rep[:, c, :], scratch[:, 0, 0:P], bias_in[:, 0, c:c + 1], None, ALU.mult)
                last = dve.tensor_scalar(bv2_rep[:, c, :], scratch[:, 0, 0:P], bias_in[:, 2, c:c + 1], 2.0, ALU.mult, ALU.mult)
            last.then_inc(bias_step, 1)
            const(dve.tensor_tensor(neg_gw[:, :], sig[:, :], sig[:, :], ALU.mult))
            const(dve.tensor_scalar(neg_gw[:, :], neg_gw[:, :], -2.0, None, ALU.mult))
            dve.reciprocal(neg_gw[:, :], neg_gw[:, :])
            for t in range(TT):
                last = dve.tensor_scalar(hcol[:, t:t + 1], pi[:, 1:2], float(t * SIDE // TT), None, ALU.add)
            const(last)
            masks = [(row_mask[:, :], P, 2, pi[:, 2:3], 1, pi[:, 1:2])]
            masks += [(col_mask[:, t, :], TOKENS, 1, hcol[:, t:t + 1], 2, pi[:, 2:3]) for t in range(TT)]
            for mask, width, along, mine, across, same in masks:
                inside, dist = scratch[:, 0, 0:width], scratch[:, 1, 0:width]
                dve.tensor_scalar(dist, ji[:, along, 0:width], mine, None, ALU.subtract)
                const(dve.tensor_scalar(inside, ji[:, across, 0:width], same, None, ALU.is_equal))
                const(dve.tensor_tensor(dist, dist, inside, ALU.mult))
                const(dve.tensor_tensor(dist, dist, dist, ALU.mult))
                dve.tensor_scalar(inside, inside, -1.0, FAR, ALU.add, ALU.mult)
                const(dve.tensor_scalar(dist, dist, neg_gw[:, :], None, ALU.mult))
                const(dve.tensor_tensor(mask, dist, inside, ALU.add))
            take_kv(0, 1)
            take_kv(0, 3)
            take_q(0)
            dve.wait_ge(wot_ready, 1)
            dve.tensor_copy(wo_t[:, :, :].rearrange("p c n -> p (c n)"), trans_bank[:, :]).then_inc(wot_done, 1)
            for i, (lo, hi, src) in enumerate(((g_lo, g_hi, y_bank), (wvo_lo, wvo_hi, vp_bank))):
                dve.wait_ge(fold_hi_done, i + 1)
                dve.tensor_tensor(lo[:, :, :].rearrange("p c n -> p (c n)"), src[:, :],
                                  hi[:, :, :].rearrange("p c n -> p (c n)").bitcast(FP32), ALU.subtract).then_inc(fold_split, 1)
            dve.wait_ge(fold_ready, 3)
            dve.tensor_copy(r_col[:, :], stat_bank[:, 8:8 + CC])
            dve.tensor_copy(c1[:, :], stat_bank[:, 10:10 + CC]).then_inc(bias_step, 1)
            dve.tensor_copy(s0[:, :], stat_bank[:, 12:13]).then_inc(bias_step, 1)
            dve.tensor_tensor(bias_out[:, :], t_bank[:, 0:DIM], bo_row[:, :], ALU.add).then_inc(bias_step, 1)

            attention(0, False, True)
            project(0, True)
            with dve.Fori(1, BATCHES - 1) as b:
                attention(b, True, True)
                project(b, True)
            attention(BATCHES - 1, True, False)
            project(BATCHES - 1, False)
            logits(BATCHES - 1)
            maxima(BATCHES - 1)
            weights(BATCHES - 1)
            split_attn(BATCHES - 1)
            final_sum(BATCHES - 1)

        @block.tensor
        def _(pe):
            def product(dst, pairs):
                passes = [(a, b) for (a_hi, a_lo), (b_hi, b_lo) in pairs
                          for a, b in ((a_hi, b_hi), (a_hi, b_lo), (a_lo, b_hi))]
                for i, (a, b) in enumerate(passes):
                    last = pe.matmul(dst, a, b, start=(i == 0), stop=(i == len(passes) - 1))
                return last

            def transpose_tokens(src):
                for c in range(CC):
                    for t in range(TT):
                        last = pe.transpose(trans_bank[:, c * TOKENS + t * P:c * TOKENS + (t + 1) * P],
                                            src[:, t, c * P:(c + 1) * P], ident[:, :])
                return last

            def group_mean(k, b):
                pe.wait_ge(stat_in[k], 2 * b + 1)
                pe.matmul(stat_bank[:, 0:CC], group_avg[:, :], mv[k][:, :, 0], start=True, stop=True).then_inc(stat_sum[k], 1)

            def group_variance(k, b):
                pe.wait_ge(stat_in[k], 2 * b + 2)
                pe.matmul(stat_bank[:, CC:2 * CC], group_avg[:, :], shift[k][:, 0, :], start=True, stop=True).then_inc(stat_sum[k], 1)

            def project_kv(b, i):
                axis, t = 1 - i // TT, i % TT
                if i == 0:
                    pe.wait_ge(xn_split[0], b + 1)
                if i == 3:
                    pe.wait_ge(o_lo_done, 2 * b)
                if i == TT:
                    pe.wait_ge(turned, b + 1)
                hi, lo = (xt_hi, xt_lo) if axis == 0 else (xn_hi[0], xn_lo[0])
                product(proj_bank[i][:, :],
                        [((hi[:, c, t * P:(t + 1) * P], lo[:, c, t * P:(t + 1) * P]),
                          (wqkv_hi[:, axis, c, DIM:3 * DIM], wqkv_lo[:, axis, c, DIM:3 * DIM])) for c in range(CC)]
                        ).then_inc(kv_proj, 1)

            def project_q(b, i):
                axis = 1 - i
                hi, lo = (xt_hi, xt_lo) if axis == 0 else (xn_hi[0], xn_lo[0])
                if i == 1:
                    pe.wait_ge(kv_act, 2 * b + 1)
                for m in range(CC):
                    last = product(q_bank[i][:, m * TOKENS:(m + 1) * TOKENS],
                                   [((wqkv_hi[:, axis, c, m * P:(m + 1) * P], wqkv_lo[:, axis, c, m * P:(m + 1) * P]),
                                     (hi[:, c, :], lo[:, c, :])) for c in range(CC)])
                last.then_inc(q_proj, 1)

            def carry():
                pe.sem_inc(pe_waited, 1)

            def key_value(b, n):
                axis, t = tile_of(n)
                if n == 0:
                    pe.wait_ge(kv_act, 2 * (b + 1))
                    pe.wait_ge(kv_dve, 2 * (b + 1))
                    pe.wait_ge(q_act, b + 1)
                    pe.wait_ge(q_dve, b + 1)
                if n == 1:
                    pe.wait_ge(logits_done, b)
                if n >= 2:
                    pe.wait_ge(kv_masked, TILES * b + n - 1)
                for quad in range(QUADS):
                    rows = slice(QUAD * quad, QUAD * (quad + 1))
                    if quad >= 2:
                        pe.wait_ge(kv_ready, QUADS * TILES * b + QUADS * n + quad - 1)
                    carry()
                    for c in range(CC):
                        first = (quad // 2 * CC + c) * 2 * PAIR
                        for pair in range(PAIRS):
                            channels = slice(c * P + pair * PAIR, c * P + (pair + 1) * PAIR)
                            last = pe.matmul(kv_bank[n % 2][quad % 2][pair * PAIR:(pair + 1) * PAIR, first:first + 2 * PAIR],
                                             k[rows, axis, t, channels], v[rows, axis, t, :, channels], start=True, stop=True)
                    last.then_inc(kv_ready, 1)

            def queries(b, n):
                axis, t = tile_of(n)
                pe.wait_ge(kv_masked, TILES * b + n + 1)
                if n == 0:
                    pe.wait_ge(t_lo_done, b)
                    pe.wait_ge(vp_lo_done, b)
                else:
                    pe.wait_ge(o_done, TILES * b + n)
                for i, pair in enumerate((0, 2, 1, 3)):
                    rows = slice(PAIR * pair, PAIR * (pair + 1))
                    if i >= 2:
                        pe.wait_ge(pair_done, 2 * (TILES * b + n) + i - 1)
                    carry()
                    for c in range(CC):
                        for quad in range(QUADS):
                            half = qkv_bank[pair // 2][quad * QUAD:(quad + 1) * QUAD, 0:2 * P].rearrange("p (s a) -> p s a", s=2)
                            at = c * 2 * PAIR + pair % 2 * PAIR
                            first = t * P + quad * QUAD
                            last = pe.matmul(half[:, :, at:at + PAIR], q[rows, axis, c, first:first + QUAD],
                                             kv[rows, n % 2, quad % 2 * 2 + quad // 2, c, :, :], start=True, stop=True)
                    if i < 2:
                        last.then_inc(pair_done, 1)
                last.then_inc(o_ready, 1)

            def transpose_output(b, axis):
                pe.wait_ge(o_done, TILES * b + TT * (axis + 1))
                pe.wait_ge(kv_masked, TILES * b + 3)
                for c in range(CC):
                    for t in range(TT):
                        last = pe.transpose(ot_bank[axis][:, c * TOKENS + t * P:c * TOKENS + (t + 1) * P],
                                            o_tok[:, axis, t, c * P:(c + 1) * P], ident[:, :])
                last.then_inc(ot_ready, 1)

            def scores(b):
                pe.wait_ge(t_lo_done, b + 1)
                pe.wait_ge(x1_ready, b + 1)
                for t in range(TT):
                    last = product(s_bank[:, t * TOKENS:(t + 1) * TOKENS],
                                   [((t_hi[:, c, t * P:(t + 1) * P], t_lo[:, c, t * P:(t + 1) * P]),
                                     (xn_hi[1][:, c, :], xn_lo[1][:, c, :])) for c in range(CC)])
                last.then_inc(s_ready, 1)

            def transpose_weights(b):
                pe.wait_ge(attn_ready, b + 1)
                pe.wait_ge(xn_ready[1], b + 1)
                for j in range(TT):
                    for i in range(TT):
                        last = pe.transpose(trans_bank[:, (j * TT + i) * P:(j * TT + i + 1) * P],
                                            attn[:, i, j * P:(j + 1) * P], ident[:, :])
                last.then_inc(at_ready, 1)

            def weighted_values(b):
                pe.wait_ge(at_lo_done, b + 1)
                pe.wait_ge(vp_lo_done, b + 1)
                for i in range(TT):
                    last = product(pv_bank[:, i * DIM:(i + 1) * DIM],
                                   [((at_hi[:, j, i, :], at_lo[:, j, i, :]), (vp_hi[:, j, :], vp_lo[:, j, :])) for j in range(TT)])
                last.then_inc(pv_ready, 1)

            def transpose_x(b):
                pe.wait_ge(x_loaded, 16 * (b + 1))
                transpose_tokens(x_in).then_inc(xt_ready[0], 1)

            def attention(b, has_prev, has_next):
                key_value(b, 0)
                key_value(b, 1)
                queries(b, 0)
                if has_prev:
                    transpose_weights(b - 1)
                key_value(b, 2)
                if has_prev:
                    weighted_values(b - 1)
                queries(b, 1)
                if has_next:
                    pe.wait_ge(out_ready, b)
                    transpose_x(b + 1)
                key_value(b, 3)
                if has_next:
                    group_mean(0, b + 1)
                queries(b, 2)
                if has_next:
                    group_variance(0, b + 1)
                transpose_output(b, 0)
                queries(b, 3)
                transpose_output(b, 1)

            def project(b, has_next):
                pe.wait_ge(o_lo_done, 2 * (b + 1))
                pe.wait_ge(out_ready, b)
                for t in range(TT):
                    last = product(y_bank[:, t * DIM:(t + 1) * DIM],
                                   [((o_hi[:, axis, c, t * P:(t + 1) * P], o_lo[:, axis, c, t * P:(t + 1) * P]),
                                     (wout_hi[:, axis, c, :], wout_lo[:, axis, c, :])) for axis in range(2) for c in range(CC)])
                last.then_inc(y_ready, 1)
                if has_next:
                    project_kv(b + 1, 0)
                    project_kv(b + 1, 1)
                pe.wait_ge(x1_ready, b + 1)
                if has_next:
                    pe.wait_ge(xn_ready[0], b + 2)
                transpose_tokens(x1).then_inc(xt_ready[1], 1)
                if has_next:
                    project_kv(b + 1, 2)
                group_mean(1, b)
                if has_next:
                    project_kv(b + 1, 3)
                group_variance(1, b)
                if has_next:
                    project_q(b + 1, 0)
                    project_q(b + 1, 1)
                if has_next:
                    pe.wait_ge(kv_dve, 2 * (b + 1) + 1)
                pe.wait_ge(xn_split[1], b + 1)
                for m in range(CC):
                    last = product(t_bank[:, m * TOKENS:(m + 1) * TOKENS],
                                   [((g_hi[:, c, m * P:(m + 1) * P], g_lo[:, c, m * P:(m + 1) * P]),
                                     (xn_hi[1][:, c, :], xn_lo[1][:, c, :])) for c in range(CC)])
                last.then_inc(t_ready, 1)
                pe.wait_ge(coef_ready[1], b + 1)
                for t in range(TT):
                    for c in range(CC):
                        last = pe.matmul(stat_bank[:, 2 * CC + t:2 * CC + t + 1], xn[1][:, c, t * P:(t + 1) * P],
                                         r_col[:, c:c + 1], start=(c == 0), stop=(c == CC - 1))
                last.then_inc(row_ready, 1)
                if has_next:
                    pe.wait_ge(kv_act, 2 * (b + 1) + 2)
                for t in range(TT):
                    last = product(vp_bank[:, t * DIM:(t + 1) * DIM],
                                   [((xn_hi[1][:, c, t * P:(t + 1) * P], xn_lo[1][:, c, t * P:(t + 1) * P]),
                                     (wvo_hi[:, c, :], wvo_lo[:, c, :])) for c in range(CC)])
                last.then_inc(vp_ready, 1)
                scores(b)
                pe.wait_ge(row_done, b + 1)

            pe.wait_ge(consts_ready, 1)
            transpose_x(0)
            group_mean(0, 0)
            group_variance(0, 0)
            pe.wait_ge(w_split, 1)
            project_kv(0, 0)
            project_kv(0, 1)
            pe.wait_ge(w_split, 2)
            project_kv(0, 2)
            project_kv(0, 3)
            project_q(0, 0)
            project_q(0, 1)

            pe.wait_ge(l1_loaded, 4 * 16)
            pe.wait_ge(kv_act, 2)
            pe.wait_ge(kv_dve, 2)
            pe.wait_ge(xn_ready[0], 1)
            for e in range(CC):
                for o in range(CC):
                    last = pe.transpose(trans_bank[:, e * DIM + o * P:e * DIM + (o + 1) * P], wl1[:, 3, o, e * P:(e + 1) * P], ident[:, :])
            last.then_inc(wot_ready, 1)
            for m in range(CC):
                for e in range(CC):
                    last = pe.matmul(y_bank[:, m * DIM:(m + 1) * DIM], wl1[:, 0, e, m * P:(m + 1) * P], wl1[:, 1, e, :],
                                     start=(e == 0), stop=(e == CC - 1))
            last.then_inc(fold_ready, 1)
            pe.wait_ge(wot_done, 1)
            for m in range(CC):
                for e in range(CC):
                    last = pe.matmul(vp_bank[:, m * DIM:(m + 1) * DIM], wl1[:, 2, e, m * P:(m + 1) * P], wo_t[:, e, :],
                                     start=(e == 0), stop=(e == CC - 1))
            last.then_inc(fold_ready, 1)
            pe.wait_ge(bias_step, 2)
            for i, (weight, vector) in enumerate(((0, 1), (1, 0))):
                for m in range(CC):
                    for e in range(CC):
                        pe.matmul(stat_bank[:, 8 + 2 * i + m:9 + 2 * i + m], wl1[:, weight, e, m * P:(m + 1) * P],
                                  bias_in[:, vector, e:e + 1], start=(e == 0), stop=(e == CC - 1))
            for e in range(CC):
                pe.matmul(stat_bank[:, 12:13], bq_rep[:, e, :], bias_in[:, 1, e:e + 1], start=(e == 0), stop=(e == CC - 1))
            for e in range(CC):
                last = pe.matmul(t_bank[:, 0:DIM], bv2_rep[:, e, :], wo_t[:, e, :], start=(e == 0), stop=(e == CC - 1))
            last.then_inc(fold_ready, 1)
            pe.wait_ge(w_split, 3)
            pe.wait_ge(fold_split, 2)
            pe.wait_ge(bias_step, 5)

            attention(0, False, True)
            project(0, True)
            with pe.Fori(1, BATCHES - 1) as b:
                attention(b, True, True)
                project(b, True)
            attention(BATCHES - 1, True, False)
            project(BATCHES - 1, False)
            transpose_weights(BATCHES - 1)
            weighted_values(BATCHES - 1)


_INS = ['x', 'L0_conv_w_qkv0', 'L0_conv_w_out0', 'L0_conv_w_qkv1', 'L0_conv_w_out1', 'L1_conv_Wq', 'L1_conv_bq',
        'L1_conv_Wk', 'L1_conv_bk', 'L1_conv_Wv', 'L1_conv_bv', 'L1_conv_Wo', 'L1_conv_bo', 'L1_conv_sigma']
_OUTS = [((8, 16, 16, 256), 'float32')]


def kernel(**inputs):
    import numpy as _np
    import concourse.bacc as _bacc
    from concourse import mybir as _mybir
    from concourse.bass_utils import run_bass_kernel_spmd as _run

    nc = _bacc.Bacc("TRN2", target_bir_lowering=False, num_devices=1)
    arrays, args = {}, []
    for name in _INS:
        a = _np.ascontiguousarray(inputs[name])
        arrays[f"in_{name}_dram"] = a
        args.append(nc.dram_tensor(f"in_{name}_dram", a.shape, _mybir.dt.from_np(a.dtype), kind="ExternalInput").ap())
    for i, (shape, dtype) in enumerate(_OUTS):
        dt = _mybir.dt.from_np(_np.dtype(dtype))
        args.append(nc.dram_tensor(f"out_{i}_dram", shape, dt, kind="ExternalOutput").ap())
    build(nc, *args)
    r = _run(nc, [arrays], core_ids=[0])
    return r.results[0]["out_0_dram"]
```

```python
import concourse.bass as bass
from concourse import mybir
from contextlib import ExitStack

FP32 = mybir.dt.float32
FP32R = mybir.dt.float32r
INT32 = mybir.dt.int32
ALU = mybir.AluOpType
ACT = mybir.ActivationFunctionType
AX = mybir.AxisListType

BATCHES, SIDE, DIM = 8, 16, 256
TOKENS = SIDE * SIDE
P = 128
TT = TOKENS // P
CC = DIM // P
HEAD = 16
GROUP = 8
EPS = 1e-5
QUAD = 32
QUADS = P // QUAD
ACT_KV = 3
TILES = 2 * TT
PAIR = 32
PAIRS = P // PAIR
FOUR = 2 * PAIR
HALVES = P // FOUR
SEQS = P // SIDE
FAR = 1.0e30


def tile_of(n):
    return 1 - n // TT, n % TT


def build(nc, x, w_qkv0, w_out0, w_qkv1, w_out1, wq, bq, wk, bk, wv, bv, wo, bo, sigma, out):
    with ExitStack() as ctx:
        def sb(name, shape, dt=FP32):
            return ctx.enter_context(nc.sbuf_tensor(name, shape, dt))

        def sem(name):
            return ctx.enter_context(nc.semaphore(name))

        wqkv_in = sb("wqkv_in", [P, 2, CC, 3 * DIM])
        wqkv_hi = sb("wqkv_hi", [P, 2, CC, 3 * DIM], FP32R)
        wqkv_lo = sb("wqkv_lo", [P, 2, CC, 3 * DIM], FP32R)
        wout_in = sb("wout_in", [P, 2, CC, DIM])
        wout_hi = sb("wout_hi", [P, 2, CC, DIM], FP32R)
        wout_lo = sb("wout_lo", [P, 2, CC, DIM], FP32R)
        wl1 = sb("wl1", [P, 4, CC, DIM])
        wo_t = sb("wo_t", [P, CC, DIM])
        g_hi = sb("g_hi", [P, CC, DIM], FP32R)
        g_lo = sb("g_lo", [P, CC, DIM], FP32R)
        wvo_hi = sb("wvo_hi", [P, CC, DIM], FP32R)
        wvo_lo = sb("wvo_lo", [P, CC, DIM], FP32R)
        bias_in = sb("bias_in", [P, 3, CC])
        bq_rep = sb("bq_rep", [P, CC, P])
        bv2_rep = sb("bv2_rep", [P, CC, P])
        bo_row = sb("bo_row", [P, DIM])
        bias_out = sb("bias_out", [P, DIM])
        c1 = sb("c1", [P, CC])
        r_col = sb("r_col", [P, CC])
        s0 = sb("s0", [P, 1])
        sig = sb("sig", [P, 1])
        neg_gw = sb("neg_gw", [P, 1])
        iota_row = sb("iota_row", [P, 1], INT32)
        iota_j = sb("iota_j", [P, 4, TOKENS], INT32)
        ji = sb("ji", [P, 4, TOKENS])
        part_i = sb("part_i", [P, 4], INT32)
        pi = sb("pi", [P, 4])
        par_i = sb("par_i", [P, 1], INT32)
        head_scale = sb("head_scale", [P, FOUR // HEAD])
        head_i = sb("head_i", [P, 1], INT32)
        head_f = sb("head_f", [P, 1])
        parity = sb("parity", [P, 2])
        ident = sb("ident", [P, P])
        group_avg = sb("group_avg", [P, P])
        block_mask = sb("block_mask", [P, FOUR])
        row_mask = sb("row_mask", [P, P])
        col_mask = sb("col_mask", [P, TT, TOKENS])
        image_row = sb("image_row", [P, TT])
        scratch = sb("scratch", [P, 2, TOKENS])
        gate = sb("gate", [P, 1])
        minus_half = sb("minus_half", [P, CC])
        x_in = sb("x_in", [P, TT, DIM])
        x_res = sb("x_res", [P, TT, DIM])
        moments = [sb(f"moments{k}", [P, CC, 6]) for k in range(2)]
        mv = [sb(f"mv{k}", [P, CC, 2]) for k in range(2)]
        gmean = [sb(f"gmean{k}", [P, CC]) for k in range(2)]
        shift = [sb(f"shift{k}", [P, 2, CC]) for k in range(2)]
        var_eps = [sb(f"var_eps{k}", [P, CC]) for k in range(2)]
        rstd = [sb(f"rstd{k}", [P, CC]) for k in range(2)]
        nbias = [sb(f"nbias{k}", [P, CC]) for k in range(2)]
        xn = [sb(f"xn{k}", [P, CC, TOKENS]) for k in range(2)]
        xn_hi = [sb(f"xn_hi{k}", [P, CC, TOKENS], FP32R) for k in range(2)]
        xn_lo = [sb(f"xn_lo{k}", [P, CC, TOKENS], FP32R) for k in range(2)]
        xt_hi = sb("xt_hi", [P, CC, TOKENS], FP32R)
        xt_lo = sb("xt_lo", [P, CC, TOKENS], FP32R)
        k_v = sb("k_v", [P, 2, TT, 2, DIM])
        v_wide = sb("v_wide", [P, 2, TT, SEQS, DIM])
        q = sb("q", [P, 2, CC, TOKENS])
        kv = sb("kv", [P, 2, CC, SEQS, 2, PAIR])
        o_even = sb("o_even", [P, CC, HALVES, FOUR])
        o_tok = sb("o_tok", [P, 2, TT, DIM])
        o_hi = sb("o_hi", [P, 2, CC, TOKENS], FP32R)
        o_lo = sb("o_lo", [P, 2, CC, TOKENS], FP32R)
        x1 = sb("x1", [P, TT, DIM])
        x1b = sb("x1b", [P, TT, DIM])
        t_hi = sb("t_hi", [P, CC, TOKENS], FP32R)
        t_lo = sb("t_lo", [P, CC, TOKENS], FP32R)
        vp_hi = sb("vp_hi", [P, TT, DIM], FP32R)
        vp_lo = sb("vp_lo", [P, TT, DIM], FP32R)
        row_term = sb("row_term", [P, TT])
        log_row = sb("log_row", [P, TT, P])
        log_col = sb("log_col", [P, TT, TOKENS])
        neg_max = sb("neg_max", [P, 2, TT])
        exp_row = sb("exp_row", [P, TT, P])
        exp_col = sb("exp_col", [P, TT, TOKENS])
        exp_sum = sb("exp_sum", [P, 2, TT])
        inv_sum = sb("inv_sum", [P, 2, TT])
        row_weights = sb("row_weights", [P, TT, P])
        attn = sb("attn", [P, TT, TOKENS])
        at_hi = sb("at_hi", [P, TT, TT, P], FP32R)
        at_lo = sb("at_lo", [P, TT, TT, P], FP32R)
        y_out = sb("y_out", [P, TT, DIM])
        bank = [ctx.enter_context(nc.psum_tensor(f"bank{i}", [P, 512], FP32)) for i in range(8)]
        trans_bank, stat_bank = bank[0], bank[1]
        kv_bank = bank[2:4]
        qkv_bank = bank[4:6]
        ot_bank = bank[2:4]
        y_bank, t_bank = bank[6], bank[6]
        proj_bank, q_bank = [bank[0], bank[2], bank[4], bank[5]], [bank[4], bank[5]]
        vp_bank, at_bank, pv_bank = bank[7], bank[7], bank[7]

        x_loaded, stored = sem("x_loaded"), sem("stored")
        w_loaded = [sem(f"w_loaded{i}") for i in range(2)]
        wout_loaded, l1_loaded, bias_loaded = sem("wout_loaded"), sem("l1_loaded"), sem("bias_loaded")
        iota_done, const_step, consts_ready = sem("iota_done"), sem("const_step"), sem("consts_ready")
        head_ready = sem("head_ready")
        w_hi_done, w_split = sem("w_hi_done"), sem("w_split")
        fold_ready, fold_hi_done, fold_split = sem("fold_ready"), sem("fold_hi_done"), sem("fold_split")
        wot_ready, wot_done, bias_step = sem("wot_ready"), sem("wot_done"), sem("bias_step")
        xt_ready = [sem(f"xt_ready{k}") for k in range(2)]
        norm_step = [sem(f"norm_step{k}") for k in range(2)]
        stat_in = [sem(f"stat_in{k}") for k in range(2)]
        stat_sum = [sem(f"stat_sum{k}") for k in range(2)]
        var_ready = [sem(f"var_ready{k}") for k in range(2)]
        rstd_ready = [sem(f"rstd_ready{k}") for k in range(2)]
        coef_ready = [sem(f"coef_ready{k}") for k in range(2)]
        xn_ready = [sem(f"xn_ready{k}") for k in range(2)]
        xn_hi_done = [sem(f"xn_hi_done{k}") for k in range(2)]
        xn_split = [sem(f"xn_split{k}") for k in range(2)]
        res_ready, turned = sem("res_ready"), sem("turned")
        kv_proj, kv_act, kv_dve = sem("kv_proj"), sem("kv_act"), sem("kv_dve")
        v_cleared, v_placed = sem("v_cleared"), [sem(f"v_placed{axis}") for axis in range(2)]
        q_proj, q_taken = sem("q_proj"), sem("q_taken")
        pe_waited = sem("pe_waited")
        kv_ready, o_ready = sem("kv_ready"), sem("o_ready")
        kv_masked, kv_masked_act = sem("kv_masked"), sem("kv_masked_act")
        o_even_done, o_done, ot_ready = sem("o_even_done"), sem("o_done"), sem("ot_ready")
        o_hi_done, o_lo_done = sem("o_hi_done"), sem("o_lo_done")
        y_ready, x1_ready, x1b_ready = sem("y_ready"), sem("x1_ready"), sem("x1b_ready")
        t_ready, t_hi_done, t_lo_done = sem("t_ready"), sem("t_hi_done"), sem("t_lo_done")
        row_ready, row_done = sem("row_ready"), sem("row_done")
        vp_ready, vp_hi_done, vp_lo_done = sem("vp_ready"), sem("vp_hi_done"), sem("vp_lo_done")
        s_ready, logits_done, max_ready = sem("s_ready"), sem("logits_done"), sem("max_ready")
        exp_done, sums_inverted = sem("exp_done"), sem("sums_inverted")
        soft_step, attn_ready = sem("soft_step"), sem("attn_ready")
        at_ready, at_hi_done, at_lo_done = sem("at_ready"), sem("at_hi_done"), sem("at_lo_done")
        pv_ready, out_ready = sem("pv_ready"), sem("out_ready")

        x_dram = x.rearrange("b h w d -> b (h w) d")
        out_dram = out.rearrange("b h w d -> b (h w) d")

        def by_axis(ap, axis):
            return ap.rearrange("p (h w) -> p w h", h=SIDE) if axis == 0 else ap.rearrange("p (h w) -> p h w", h=SIDE)

        def masked(b, n):
            return (kv_masked_act, b + 1) if n == 1 else (kv_masked, (TILES - 1) * b + max(n, 1))

        block = ctx.enter_context(nc.Block())

        @block.sync
        def _(sp):
            def load_x(b):
                sp.dma_start(x_in[:, :, :], x_dram[bass.ds(b, 1), :, :].rearrange("a (t p) d -> p (a t) d", p=P)
                             ).then_inc(x_loaded, 16)

            def store_y(b):
                sp.wait_ge(out_ready, b + 1)
                sp.dma_start(out_dram[bass.ds(b, 1), :, :].rearrange("a (t p) d -> p (a t) d", p=P), y_out[:, :, :]
                             ).then_inc(stored, 16)

            load_x(0)
            sp.dma_start(wqkv_in[:, 1, :, :], w_qkv1.rearrange("(c p) n -> p c n", p=P)).then_inc(w_loaded[1], 16)
            for i, w in enumerate((wq, wk)):
                sp.dma_start(wl1[:, i, :, :], w.rearrange("(c p) n -> p c n", p=P)).then_inc(l1_loaded, 16)
            for i, w in enumerate((w_out0, w_out1)):
                sp.dma_start(wout_in[:, i, :, :], w.rearrange("(c p) n -> p c n", p=P)).then_inc(wout_loaded, 16)
            for i, vector in enumerate((bq, bk, bv)):
                sp.dma_start(bias_in[:, i, :], vector.rearrange("(c p) -> p c", p=P), allow_slow_non_contiguous=True).then_inc(bias_loaded, 16)
            sp.dma_start(sig[:, :], sigma.rearrange("(a n) -> a n", a=1).partition_broadcast(P)).then_inc(bias_loaded, 16)
            sp.dma_start(bo_row[:, :], bo.rearrange("(a n) -> a n", a=1).partition_broadcast(P)).then_inc(bias_loaded, 16)

            def place_v(b, axis):
                if axis == 1:
                    sp.wait_ge(kv_act, ACT_KV * b + TT)
                else:
                    sp.wait_ge(kv_dve, b + 1)
                for s in range(SEQS):
                    tokens = slice(s * SIDE, (s + 1) * SIDE)
                    sp.dma_start(v_wide[tokens, axis, :, s, :], k_v[tokens, axis, :, 1, :]).then_inc(v_placed[axis], 16)

            def next_x(b):
                sp.wait_ge(xt_ready[0], b)
                sp.wait_ge(res_ready, b)
                load_x(b)

            def batch(b, has_prev, next_batches):
                if next_batches >= 1:
                    place_v(b + 1, 1)
                if next_batches >= 2:
                    next_x(b + 2)
                if next_batches >= 1:
                    place_v(b + 1, 0)
                if has_prev:
                    store_y(b - 1)

            next_x(1)
            sp.wait_ge(v_cleared, 1)
            place_v(0, 1)
            place_v(0, 0)
            batch(0, False, 2)
            with sp.Fori(1, BATCHES - 2) as b:
                batch(b, True, 2)
            batch(BATCHES - 2, True, 1)
            batch(BATCHES - 1, True, 0)
            store_y(BATCHES - 1)
            sp.wait_ge(stored, 16 * BATCHES)

        @block.gpsimd
        def _(pool):
            pool.iota(iota_row[:, :], [[0, 1]], base=0, channel_multiplier=1).then_inc(iota_done, 1)
            for i, pattern in ((0, [[1, 256]]), (3, [[1, 32], [0, 8]]), (1, [[1, 16], [0, 16]]), (2, [[0, 16], [1, 16]])):
                pool.iota(iota_j[:, i, :], pattern, base=0, channel_multiplier=0).then_inc(iota_done, 1)

            def turn(b):
                if not (isinstance(b, int) and b == 0):
                    pool.wait_ge(q_proj, 2 * b)
                pool.wait_ge(xn_hi_done[0], b + 1)
                for c in range(CC):
                    pool.tensor_tensor(xt_lo[:, c, :].rearrange("p (w h) -> p w h", w=SIDE), by_axis(xn[0][:, c, :], 0),
                                       by_axis(xn_hi[0][:, c, :].bitcast(FP32), 0), ALU.subtract)
                for c in range(CC):
                    last = pool.tensor_copy(xt_hi[:, c, :].rearrange("p (w h) -> p w h", w=SIDE), by_axis(xn_hi[0][:, c, :], 0))
                last.then_inc(turned, 1)

            def inverse_root(k, b):
                pool.wait_ge(var_ready[k], b + 1)
                pool.tensor_tensor(rstd[k][:, :], var_eps[k][:, :], minus_half[:, :], ALU.pow).then_inc(rstd_ready[k], 1)

            pool.memset(minus_half[:, :], -0.5).then_inc(iota_done, 1)
            pool.memset(v_wide[:, :, :, :, :], 0.0).then_inc(v_cleared, 1)
            pool.wait_ge(iota_done, 6)
            inverse_root(0, 0)
            turn(0)

            def batch(b, has_prev, has_next):
                if has_next:
                    inverse_root(0, b + 1)
                    turn(b + 1)
                if has_prev:
                    weights(b - 1)
                inverse_root(1, b)
                pool.wait_ge(x1_ready, b + 1)
                pool.wait_ge(out_ready, b)
                for t in range(TT):
                    last = pool.tensor_tensor(x1b[:, t, :], x1[:, t, :], bias_out[:, :], ALU.add)
                last.then_inc(x1b_ready, 1)

            def weights(b):
                pool.wait_ge(sums_inverted, b + 1)
                pool.tensor_tensor(attn[:, :, :], exp_col[:, :, :], inv_sum[:, 1, :].unsqueeze(2).broadcast_to([P, TT, TOKENS]), ALU.mult)
                pool.tensor_tensor(row_weights[:, :, :], exp_row[:, :, :], inv_sum[:, 0, :].unsqueeze(2).broadcast_to([P, TT, P]),
                                   ALU.mult).then_inc(soft_step, 1)
                pool.wait_ge(soft_step, b + 1)
                for t in range(TT):
                    own = attn[:, t, t * P:(t + 1) * P]
                    last = pool.tensor_tensor(own, row_weights[:, t, :], own, ALU.add)
                last.then_inc(attn_ready, 1)

            pool.wait_ge(bias_step, 5)
            batch(0, False, True)
            with pool.Fori(1, BATCHES - 1) as b:
                batch(b, True, True)
            batch(BATCHES - 1, True, False)

        @block.scalar
        def _(act):
            act.dma_start(wqkv_in[:, 0, :, :], w_qkv0.rearrange("(c p) n -> p c n", p=P)).then_inc(w_loaded[0], 16)
            for i, w in ((3, wo), (2, wv)):
                act.dma_start(wl1[:, i, :, :], w.rearrange("(c p) n -> p c n", p=P)).then_inc(l1_loaded, 16)

            def copy_residual(b):
                act.wait_ge(x_loaded, 16 * (b + 1))
                act.wait_ge(x1_ready, b)
                act.activation(x_res[:, :, :], x_in[:, :, :], ACT.Copy).then_inc(res_ready, 1)

            def normalise(k, b):
                act.wait_ge(coef_ready[k], b + 1)
                act.wait_ge(xn_split[k], b)
                if k == 0:
                    act.wait_ge(turned, b)
                for c in range(CC):
                    last = act.activation(xn[k][:, c, :], trans_bank[:, c * TOKENS:(c + 1) * TOKENS], ACT.Identity,
                                          bias=nbias[k][:, c:c + 1], scale=rstd[k][:, c:c + 1])
                last.then_inc(xn_ready[k], 1)

            def take_kv(b, i):
                axis, t = tile_of(i)
                src = proj_bank[i]
                act.wait_ge(kv_proj, TILES * b + i + 1)
                act.activation(k_v[:, axis, t, :, :].rearrange("p i d -> p (i d)"), src[:, :], ACT.Copy).then_inc(kv_act, 1)

            def take_q(b, i):
                act.wait_ge(q_proj, 2 * b + i + 1)
                act.activation(q[:, 1 - i, :, :].rearrange("p c n -> p (c n)"), q_bank[i][:, :], ACT.Copy).then_inc(q_taken, 1)

            def mask_kv(b):
                act.wait_ge(kv_ready, TILES * b + 2)
                for head in range(FOUR // HEAD):
                    own = slice(head % 2 * HEAD, (head % 2 + 1) * HEAD)
                    last = act.activation(kv[:, 1, :, :, head // 2, own].rearrange("p c s e -> p (c s) e"),
                                          kv_bank[1][:, :].rearrange("p (a e) -> p a e", e=PAIR)[:, :, own], ACT.Copy,
                                          scale=head_scale[:, head:head + 1])
                last.then_inc(kv_masked_act, 1)

            def take_even(b, n):
                act.wait_ge(o_ready, TILES * b + n + 1)
                for r in range(HALVES):
                    src = qkv_bank[r][:, :CC * 2 * FOUR].rearrange("p (c s a) -> p c s a", c=CC, s=2)
                    last = act.activation(o_even[:, :, r, :], src[:, :, 0, :], ACT.Copy, scale=parity[:, 0:1])
                last.then_inc(o_even_done, 1)

            def split_o(b, axis):
                act.wait_ge(ot_ready, 2 * b + 2 - axis)
                for c in range(CC):
                    last = act.activation(by_axis(o_hi[:, axis, c, :], axis),
                                          ot_bank[1 - axis][:, c * TOKENS:(c + 1) * TOKENS].rearrange("p (s i) -> p s i", s=SIDE), ACT.Copy)
                last.then_inc(o_hi_done, 1)

            def exponentials(b, t):
                act.wait_ge(max_ready, b + 1)
                act.activation(exp_row[:, t, :], log_row[:, t, :], ACT.Exp, bias=neg_max[:, 0, t:t + 1],
                               accum_out=exp_sum[:, 0, t:t + 1])
                act.activation(exp_col[:, t, :], log_col[:, t, :], ACT.Exp, bias=neg_max[:, 1, t:t + 1],
                               accum_out=exp_sum[:, 1, t:t + 1]).then_inc(exp_done, 1)

            def split_attn(b):
                act.wait_ge(at_ready, b + 1)
                act.activation(at_hi[:, :, :, :].rearrange("p j i q -> p (j i q)"), at_bank[:, :], ACT.Copy).then_inc(at_hi_done, 1)

            def high_t(b):
                act.wait_ge(t_ready, b + 1)
                for c in range(CC):
                    last = act.activation(t_hi[:, c, :], t_bank[:, c * TOKENS:(c + 1) * TOKENS], ACT.Identity, bias=c1[:, c:c + 1])
                last.then_inc(t_hi_done, 1)

            def high_values(b):
                act.wait_ge(vp_ready, b + 1)
                act.activation(vp_hi[:, :, :].rearrange("p t d -> p (t d)"), vp_bank[:, :], ACT.Copy).then_inc(vp_hi_done, 1)

            def attention(b, has_prev, has_next):
                mask_kv(b)
                if has_prev:
                    high_t(b - 1)
                take_even(b, 0)
                if has_prev:
                    high_values(b - 1)
                take_even(b, 1)
                if has_next:
                    normalise(0, b + 1)
                split_o(b, 1)
                take_even(b, 2)
                if has_next:
                    take_kv(b + 1, 0)
                take_even(b, 3)
                if has_next:
                    take_kv(b + 1, 1)
                split_o(b, 0)
                if has_prev:
                    exponentials(b - 1, 0)

            def project(b, has_prev, has_next):
                if has_prev:
                    exponentials(b - 1, 1)
                if has_next:
                    take_kv(b + 1, 2)
                    copy_residual(b + 1)
                if has_prev:
                    split_attn(b - 1)
                if has_next:
                    take_q(b + 1, 0)
                normalise(1, b)
                if has_next:
                    take_q(b + 1, 1)

            def high_qkv(axis):
                act.wait_ge(w_loaded[axis], 16)
                act.activation(wqkv_hi[:, axis, :, 0:DIM], wqkv_in[:, axis, :, 0:DIM], ACT.Copy, scale=DIM ** -0.5)
                act.activation(wqkv_hi[:, axis, :, DIM:3 * DIM], wqkv_in[:, axis, :, DIM:3 * DIM], ACT.Copy).then_inc(w_hi_done, 1)

            act.wait_ge(const_step, 1)
            act.activation(head_f[:, :], head_i[:, :], ACT.Copy).then_inc(head_ready, 1)
            high_qkv(1)
            copy_residual(0)
            high_qkv(0)
            normalise(0, 0)
            act.wait_ge(consts_ready, 2)
            act.wait_ge(wout_loaded, 2 * 16)
            act.activation(wout_hi[:, :, :, :].rearrange("p a c n -> p (a c n)"),
                           wout_in[:, :, :, :].rearrange("p a c n -> p (a c n)"), ACT.Copy).then_inc(w_hi_done, 1)

            def high_fold(dst, step):
                act.wait_ge(fold_ready, step)
                act.activation(dst[:, :, :].rearrange("p c n -> p (c n)"), y_bank[:, :], ACT.Copy).then_inc(fold_hi_done, 1)

            high_fold(g_hi, 1)
            for i in range(ACT_KV):
                take_kv(0, i)
            take_q(0, 0)
            take_q(0, 1)
            high_fold(wvo_hi, 3)

            attention(0, False, True)
            project(0, False, True)
            with act.Fori(1, BATCHES - 1) as b:
                attention(b, True, True)
                project(b, True, True)
            attention(BATCHES - 1, True, False)
            project(BATCHES - 1, True, False)
            high_t(BATCHES - 1)
            high_values(BATCHES - 1)
            exponentials(BATCHES - 1, 0)
            exponentials(BATCHES - 1, 1)
            split_attn(BATCHES - 1)

        @block.vector
        def _(dve):
            steps = [0]

            def const(inst):
                inst.then_inc(const_step, 1)
                steps[0] += 1
                dve.wait_ge(const_step, steps[0])

            dve.wait_ge(iota_done, 1)
            for i, (shift_by, keep) in enumerate(((0, 0x7f), (4, 0x7f), (0, 15), (3, 0x7f))):
                dve.tensor_scalar(part_i[:, i:i + 1], iota_row[:, :], shift_by, keep, ALU.logical_shift_right, ALU.bitwise_and)
            dve.tensor_scalar(head_i[:, :], iota_row[:, :], 4, 3, ALU.logical_shift_right, ALU.bitwise_and)
            const(dve.tensor_scalar(par_i[:, :], iota_row[:, :], 4, 1, ALU.logical_shift_right, ALU.bitwise_and))
            dve.tensor_copy(pi[:, :], part_i[:, :])
            dve.wait_ge(iota_done, 3)
            dve.tensor_copy(ji[:, 0, :], iota_j[:, 0, :])
            const(dve.tensor_copy(ji[:, 3, :], iota_j[:, 3, :]))
            dve.tensor_scalar(ident[:, :], ji[:, 0, 0:P], pi[:, 0:1], None, ALU.is_equal)
            dve.tensor_scalar(group_avg[:, :], ji[:, 3, 0:P], pi[:, 3:4], 1.0 / GROUP, ALU.is_equal, ALU.mult).then_inc(consts_ready, 1)

            def statistics(k, b):
                dve.wait_ge(xt_ready[k], b + 1)
                for c in range(CC):
                    last = dve.bn_stats(moments[k][:, c, :], trans_bank[:, c * TOKENS:(c + 1) * TOKENS])
                last.then_inc(norm_step[k], 1)
                dve.wait_ge(norm_step[k], 4 * b + 1)
                dve.memset(gate[:, :], 0.0)
                for c in range(CC):
                    last = dve.bn_aggr(mv[k][:, c, :], moments[k][:, c, :])
                last.then_inc(stat_in[k], 1)

            def spread(k, b):
                dve.wait_ge(stat_sum[k], 2 * b + 1)
                dve.tensor_copy(gmean[k][:, :], stat_bank[:, 0:CC]).then_inc(norm_step[k], 1)
                dve.wait_ge(norm_step[k], 4 * b + 2)
                dve.tensor_tensor(shift[k][:, 0, :], mv[k][:, :, 0], gmean[k][:, :], ALU.subtract).then_inc(norm_step[k], 1)
                dve.wait_ge(norm_step[k], 4 * b + 3)
                dve.tensor_tensor(shift[k][:, 1, :], shift[k][:, 0, :], shift[k][:, 0, :], ALU.mult).then_inc(norm_step[k], 1)
                dve.wait_ge(norm_step[k], 4 * b + 4)
                dve.tensor_tensor(shift[k][:, 0, :], shift[k][:, 1, :], mv[k][:, :, 1], ALU.add).then_inc(stat_in[k], 1)

            def variance(k, b):
                dve.wait_ge(stat_sum[k], 2 * b + 2)
                dve.tensor_scalar(var_eps[k][:, :], stat_bank[:, CC:2 * CC], EPS, None, ALU.add).then_inc(var_ready[k], 1)

            def coefficients(k, b):
                dve.wait_ge(rstd_ready[k], b + 1)
                dve.scalar_tensor_tensor(nbias[k][:, :], gmean[k][:, :], -1.0, rstd[k][:, :], ALU.mult, ALU.mult).then_inc(coef_ready[k], 1)

            def split_xn(k, b):
                dve.wait_ge(xn_ready[k], b + 1)
                dve.tensor_copy(xn_hi[k][:, :, :], xn[k][:, :, :]).then_inc(xn_hi_done[k], 1)
                dve.wait_ge(xn_hi_done[k], b + 1)
                dve.tensor_tensor(xn_lo[k][:, :, :], xn[k][:, :, :], xn_hi[k][:, :, :].bitcast(FP32), ALU.subtract).then_inc(xn_split[k], 1)

            def take_kv(b, i):
                axis, t = tile_of(i)
                src = proj_bank[i]
                dve.wait_ge(kv_act, ACT_KV * (b + 1))
                dve.wait_ge(kv_proj, TILES * b + i + 1)
                dve.tensor_copy(k_v[:, axis, t, :, :].rearrange("p i d -> p (i d)"), src[:, :]).then_inc(kv_dve, 1)

            def mask_kv(b, n):
                dve.wait_ge(kv_ready, TILES * b + n + 1)
                for pair in range(2):
                    last = dve.tensor_tensor(kv[:, n % 2, :, :, pair, :].rearrange("p c s e -> p (c s) e"),
                                             kv_bank[n % 2][:, :].rearrange("p (a e) -> p a e", e=PAIR),
                                             block_mask[:, pair * PAIR:(pair + 1) * PAIR].unsqueeze(1).broadcast_to([P, CC * SEQS, PAIR]),
                                             ALU.mult)
                last.then_inc(kv_masked, 1)

            def take_odd(b, n):
                axis, t = tile_of(n)
                dve.wait_ge(o_even_done, TILES * b + n + 1)
                for r in range(HALVES):
                    src = qkv_bank[r][:, :CC * 2 * FOUR].rearrange("p (c s a) -> p c s a", c=CC, s=2)
                    last = dve.scalar_tensor_tensor(
                        o_tok[:, axis, t, :].rearrange("p (c a) -> p c a", c=CC)[:, :, r * FOUR:(r + 1) * FOUR],
                        src[:, :, 1, :], parity[:, 1:2], o_even[:, :, r, :], ALU.mult, ALU.add)
                last.then_inc(o_done, 1)

            def split_o(b, axis):
                dve.wait_ge(o_hi_done, 2 * b + 2 - axis)
                for c in range(CC):
                    last = dve.tensor_tensor(by_axis(o_lo[:, axis, c, :], axis),
                                             ot_bank[1 - axis][:, c * TOKENS:(c + 1) * TOKENS].rearrange("p (s i) -> p s i", s=SIDE),
                                             by_axis(o_hi[:, axis, c, :].bitcast(FP32), axis), ALU.subtract)
                last.then_inc(o_lo_done, 1)

            def logits(b, s_bank):
                dve.wait_ge(row_done, b + 1)
                dve.wait_ge(s_ready, TT * (b + 1))
                for t in range(TT):
                    dve.scalar_tensor_tensor(log_row[:, t, :], s_bank[:, t * TOKENS + t * P:t * TOKENS + (t + 1) * P],
                                             row_term[:, t:t + 1], row_mask[:, :], ALU.add, ALU.add)
                    last = dve.scalar_tensor_tensor(log_col[:, t, :], s_bank[:, t * TOKENS:(t + 1) * TOKENS],
                                                    row_term[:, t:t + 1], col_mask[:, t, :], ALU.add, ALU.add)
                last.then_inc(logits_done, 1)

            def maxima(b):
                dve.wait_ge(logits_done, b + 1)
                dve.tensor_reduce(neg_max[:, 0, :], log_row[:, :, :], AX.X, ALU.max, negate=True)
                dve.tensor_reduce(neg_max[:, 1, :], log_col[:, :, :], AX.X, ALU.max, negate=True).then_inc(max_ready, 1)

            def split_attn(b):
                dve.wait_ge(at_hi_done, b + 1)
                dve.tensor_tensor(at_lo[:, :, :, :].rearrange("p j i q -> p (j i q)"), at_bank[:, :],
                                  at_hi[:, :, :, :].rearrange("p j i q -> p (j i q)").bitcast(FP32), ALU.subtract).then_inc(at_lo_done, 1)

            def final_sum(b):
                dve.wait_ge(pv_ready, TT * (b + 1))
                dve.wait_ge(x1b_ready, b + 1)
                dve.wait_ge(stored, 16 * b)
                dve.tensor_tensor(y_out[:, :, :].rearrange("p t d -> p (t d)"), pv_bank[:, :],
                                  x1b[:, :, :].rearrange("p t d -> p (t d)"), ALU.add).then_inc(out_ready, 1)

            def invert_sums(b):
                dve.wait_ge(exp_done, TT * (b + 1))
                dve.reciprocal(inv_sum[:, :, :], exp_sum[:, :, :]).then_inc(sums_inverted, 1)

            def last_weights():
                dve.wait_ge(sums_inverted, BATCHES)
                for t in range(TT):
                    last = dve.tensor_scalar(attn[:, t, :], exp_col[:, t, :], inv_sum[:, 1, t:t + 1], None, ALU.mult)
                last.then_inc(soft_step, 1)
                dve.wait_ge(soft_step, BATCHES)
                for t in range(TT):
                    own = attn[:, t, t * P:(t + 1) * P]
                    last = dve.scalar_tensor_tensor(own, exp_row[:, t, :], inv_sum[:, 0, t:t + 1], own, ALU.mult, ALU.add)
                last.then_inc(attn_ready, 1)

            def low_t(b):
                dve.wait_ge(t_hi_done, b + 1)
                for c in range(CC):
                    last = dve.scalar_tensor_tensor(t_lo[:, c, :], t_bank[:, c * TOKENS:(c + 1) * TOKENS], c1[:, c:c + 1],
                                                    t_hi[:, c, :].bitcast(FP32), ALU.add, ALU.subtract)
                last.then_inc(t_lo_done, 1)

            def take_row_term(b):
                dve.wait_ge(row_ready, b + 1)
                dve.tensor_scalar(row_term[:, :], stat_bank[:, 2 * CC:2 * CC + TT], s0[:, :], None, ALU.add).then_inc(row_done, 1)

            def low_values(b):
                dve.wait_ge(vp_hi_done, b + 1)
                dve.tensor_tensor(vp_lo[:, :, :].rearrange("p t d -> p (t d)"), vp_bank[:, :],
                                  vp_hi[:, :, :].rearrange("p t d -> p (t d)").bitcast(FP32), ALU.subtract).then_inc(vp_lo_done, 1)

            def attention(b, has_prev, has_next):
                if has_next:
                    statistics(0, b + 1)
                if has_prev:
                    take_row_term(b - 1)
                    low_t(b - 1)
                take_odd(b, 0)
                if has_next:
                    spread(0, b + 1)
                if has_prev:
                    low_values(b - 1)
                mask_kv(b, 2)
                if has_next:
                    variance(0, b + 1)
                take_odd(b, 1)
                if has_next:
                    coefficients(0, b + 1)
                mask_kv(b, 3)
                if has_next:
                    split_xn(0, b + 1)
                split_o(b, 1)
                take_odd(b, 2)
                if has_prev:
                    logits(b - 1, vp_bank)
                    maxima(b - 1)
                take_odd(b, 3)
                split_o(b, 0)

            def project(b, has_prev, has_next):
                if has_prev:
                    invert_sums(b - 1)
                dve.wait_ge(y_ready, b + 1)
                dve.wait_ge(res_ready, b + 1)
                dve.wait_ge(x1b_ready, b)
                dve.tensor_tensor(x1[:, :, :].rearrange("p t d -> p (t d)"), y_bank[:, :],
                                  x_res[:, :, :].rearrange("p t d -> p (t d)"), ALU.add).then_inc(x1_ready, 1)
                if has_next:
                    take_kv(b + 1, 3)
                statistics(1, b)
                if has_prev:
                    split_attn(b - 1)
                spread(1, b)
                variance(1, b)
                coefficients(1, b)
                split_xn(1, b)
                if has_next:
                    mask_kv(b + 1, 0)
                if has_prev:
                    final_sum(b - 1)

            def low_qkv(axis):
                dve.wait_ge(w_hi_done, 2 - axis)
                dve.scalar_tensor_tensor(wqkv_lo[:, axis, :, 0:DIM], wqkv_in[:, axis, :, 0:DIM], DIM ** -0.5,
                                         wqkv_hi[:, axis, :, 0:DIM].bitcast(FP32), ALU.mult, ALU.subtract)
                dve.tensor_tensor(wqkv_lo[:, axis, :, DIM:3 * DIM], wqkv_in[:, axis, :, DIM:3 * DIM],
                                  wqkv_hi[:, axis, :, DIM:3 * DIM].bitcast(FP32), ALU.subtract).then_inc(w_split, 1)

            statistics(0, 0)
            spread(0, 0)
            dve.wait_ge(iota_done, 5)
            const(dve.tensor_copy(ji[:, 1:3, :], iota_j[:, 1:3, :]))
            variance(0, 0)
            dve.wait_ge(head_ready, 1)
            dve.tensor_scalar(head_scale[:, :], ji[:, 0, 0:FOUR // HEAD], head_f[:, :], None, ALU.is_equal)
            dve.tensor_scalar(block_mask[:, :], ji[:, 1, 0:FOUR], head_f[:, :], None, ALU.is_equal)
            const(dve.tensor_copy(parity[:, 1:2], par_i[:, :]))
            dve.tensor_scalar(parity[:, 0:1], parity[:, 1:2], -1.0, 1.0, ALU.mult, ALU.add).then_inc(consts_ready, 1)
            low_qkv(1)
            coefficients(0, 0)
            split_xn(0, 0)
            low_qkv(0)
            dve.wait_ge(wot_ready, 1)
            dve.tensor_copy(wo_t[:, :, :].rearrange("p c n -> p (c n)"), kv_bank[1][:, :]).then_inc(wot_done, 1)
            dve.wait_ge(w_hi_done, 3)
            dve.tensor_tensor(wout_lo[:, :, :, :].rearrange("p a c n -> p (a c n)"), wout_in[:, :, :, :].rearrange("p a c n -> p (a c n)"),
                              wout_hi[:, :, :, :].rearrange("p a c n -> p (a c n)").bitcast(FP32), ALU.subtract).then_inc(w_split, 1)

            def low_fold(lo, hi, step):
                dve.wait_ge(fold_hi_done, step)
                dve.tensor_tensor(lo[:, :, :].rearrange("p c n -> p (c n)"), y_bank[:, :],
                                  hi[:, :, :].rearrange("p c n -> p (c n)").bitcast(FP32), ALU.subtract).then_inc(fold_split, 1)

            low_fold(g_lo, g_hi, 1)
            dve.wait_ge(bias_loaded, 5 * 16)
            dve.memset(scratch[:, 0, 0:P], 1.0).then_inc(bias_step, 1)
            dve.wait_ge(bias_step, 1)
            for c in range(CC):
                dve.tensor_scalar(bq_rep[:, c, :], scratch[:, 0, 0:P], bias_in[:, 0, c:c + 1], None, ALU.mult)
                last = dve.tensor_scalar(bv2_rep[:, c, :], scratch[:, 0, 0:P], bias_in[:, 2, c:c + 1], 2.0, ALU.mult, ALU.mult)
            last.then_inc(bias_step, 1)
            const(dve.tensor_tensor(neg_gw[:, :], sig[:, :], sig[:, :], ALU.mult))
            const(dve.tensor_scalar(neg_gw[:, :], neg_gw[:, :], -2.0, None, ALU.mult))
            dve.reciprocal(neg_gw[:, :], neg_gw[:, :])
            for t in range(TT):
                last = dve.tensor_scalar(image_row[:, t:t + 1], pi[:, 1:2], float(t * SIDE // TT), None, ALU.add)
            const(last)
            masks = [(row_mask[:, :], P, 2, pi[:, 2:3], 1, pi[:, 1:2])]
            masks += [(col_mask[:, t, :], TOKENS, 1, image_row[:, t:t + 1], 2, pi[:, 2:3]) for t in range(TT)]
            for i, (mask, width, along, mine, across, same) in enumerate(masks):
                if i == 1:
                    take_kv(0, 3)
                inside, dist = scratch[:, 0, 0:width], scratch[:, 1, 0:width]
                dve.tensor_scalar(dist, ji[:, along, 0:width], mine, None, ALU.subtract)
                const(dve.tensor_scalar(inside, ji[:, across, 0:width], same, None, ALU.is_equal))
                const(dve.tensor_tensor(dist, dist, inside, ALU.mult))
                const(dve.tensor_tensor(dist, dist, dist, ALU.mult))
                dve.tensor_scalar(inside, inside, -1.0, FAR, ALU.add, ALU.mult)
                const(dve.tensor_scalar(dist, dist, neg_gw[:, :], None, ALU.mult))
                const(dve.tensor_tensor(mask, dist, inside, ALU.add))
            dve.wait_ge(fold_ready, 2)
            dve.tensor_copy(r_col[:, :], stat_bank[:, 8:8 + CC])
            dve.tensor_copy(c1[:, :], stat_bank[:, 10:10 + CC]).then_inc(bias_step, 1)
            dve.tensor_copy(s0[:, :], stat_bank[:, 12:13]).then_inc(bias_step, 1)
            dve.tensor_tensor(bias_out[:, :], kv_bank[0][:, 0:DIM], bo_row[:, :], ALU.add).then_inc(bias_step, 1)
            low_fold(wvo_lo, wvo_hi, 2)

            mask_kv(0, 0)
            attention(0, False, True)
            project(0, False, True)
            with dve.Fori(1, BATCHES - 1) as b:
                attention(b, True, True)
                project(b, True, True)
            attention(BATCHES - 1, True, False)
            project(BATCHES - 1, True, False)
            take_row_term(BATCHES - 1)
            low_t(BATCHES - 1)
            logits(BATCHES - 1, t_bank)
            maxima(BATCHES - 1)
            low_values(BATCHES - 1)
            invert_sums(BATCHES - 1)
            last_weights()
            split_attn(BATCHES - 1)
            final_sum(BATCHES - 1)

        @block.tensor
        def _(pe):
            def product(dst, pairs, first=True, final=True):
                passes = [(a, b) for (a_hi, a_lo), (b_hi, b_lo) in pairs
                          for a, b in ((a_hi, b_hi), (a_hi, b_lo), (a_lo, b_hi))]
                for i, (a, b) in enumerate(passes):
                    last = pe.matmul(dst, a, b, start=(first and i == 0), stop=(final and i == len(passes) - 1))
                return last

            def transpose_tokens(src):
                for c in range(CC):
                    for t in range(TT):
                        last = pe.transpose(trans_bank[:, c * TOKENS + t * P:c * TOKENS + (t + 1) * P],
                                            src[:, t, c * P:(c + 1) * P], ident[:, :])
                return last

            def group_mean(k, b):
                pe.wait_ge(stat_in[k], 2 * b + 1)
                pe.matmul(stat_bank[:, 0:CC], group_avg[:, :], mv[k][:, :, 0], start=True, stop=True).then_inc(stat_sum[k], 1)

            def group_variance(k, b):
                pe.wait_ge(stat_in[k], 2 * b + 2)
                pe.matmul(stat_bank[:, CC:2 * CC], group_avg[:, :], shift[k][:, 0, :], start=True, stop=True).then_inc(stat_sum[k], 1)

            def project_kv(b, i):
                axis, t = tile_of(i)
                if i == 0:
                    pe.wait_ge(xn_split[0], b + 1)
                if i == TT:
                    pe.wait_ge(turned, b + 1)
                hi, lo = (xt_hi, xt_lo) if axis == 0 else (xn_hi[0], xn_lo[0])
                product(proj_bank[i][:, :],
                        [((hi[:, c, t * P:(t + 1) * P], lo[:, c, t * P:(t + 1) * P]),
                          (wqkv_hi[:, axis, c, DIM:3 * DIM], wqkv_lo[:, axis, c, DIM:3 * DIM])) for c in range(CC)]
                        ).then_inc(kv_proj, 1)

            def project_q(b, i):
                axis = 1 - i
                hi, lo = (xt_hi, xt_lo) if axis == 0 else (xn_hi[0], xn_lo[0])
                if i == 0:
                    pe.wait_ge(kv_act, ACT_KV * (b + 1))
                else:
                    pe.wait_ge(kv_dve, b + 1)
                for m in range(CC):
                    last = product(q_bank[i][:, m * TOKENS:(m + 1) * TOKENS],
                                   [((wqkv_hi[:, axis, c, m * P:(m + 1) * P], wqkv_lo[:, axis, c, m * P:(m + 1) * P]),
                                     (hi[:, c, :], lo[:, c, :])) for c in range(CC)])
                last.then_inc(q_proj, 1)

            def carry():
                pe.sem_inc(pe_waited, 1)

            def key_value(b, n):
                axis, t = tile_of(n)
                if t == 0:
                    pe.wait_ge(kv_act, ACT_KV * b + (ACT_KV if axis == 0 else TT))
                    pe.wait_ge(v_placed[axis], 16 * SEQS * (b + 1))
                if n >= 2:
                    pe.wait_ge(*masked(b, n - 2))
                carry()
                for c in range(CC):
                    for pair in range(PAIRS):
                        channels = slice(c * P + pair * PAIR, c * P + (pair + 1) * PAIR)
                        last = pe.matmul(kv_bank[n % 2][pair * PAIR:(pair + 1) * PAIR, c * TOKENS:(c + 1) * TOKENS],
                                         k_v[:, axis, t, 0, channels], v_wide[:, axis, t, :, channels], start=True, stop=True)
                last.then_inc(kv_ready, 1)

            def queries(b, n):
                axis, t = tile_of(n)
                pe.wait_ge(*masked(b, n))
                if n == 0:
                    pe.wait_ge(q_taken, 2 * (b + 1))
                else:
                    pe.wait_ge(o_done, TILES * b + n)
                carry()
                for r in range(HALVES):
                    rows = slice(FOUR * r, FOUR * (r + 1))
                    for c in range(CC):
                        for quad in range(QUADS):
                            first = t * P + quad * QUAD
                            last = pe.matmul(qkv_bank[r][quad * QUAD:(quad + 1) * QUAD, c * 2 * FOUR:(c + 1) * 2 * FOUR],
                                             q[rows, axis, c, first:first + QUAD],
                                             kv[rows, n % 2, c, 2 * quad:2 * quad + 2, :, :], start=True, stop=True)
                last.then_inc(o_ready, 1)

            def transpose_output(b, axis):
                pe.wait_ge(o_done, TILES * b + TT * (2 - axis))
                pe.wait_ge(*masked(b, 3 - axis))
                for c in range(CC):
                    for t in range(TT):
                        last = pe.transpose(ot_bank[1 - axis][:, c * TOKENS + t * P:c * TOKENS + (t + 1) * P],
                                            o_tok[:, axis, t, c * P:(c + 1) * P], ident[:, :])
                last.then_inc(ot_ready, 1)

            def project_out(b, axis):
                pe.wait_ge(o_lo_done, 2 * b + 2 - axis)
                for t in range(TT):
                    last = product(y_bank[:, t * DIM:(t + 1) * DIM],
                                   [((o_hi[:, axis, c, t * P:(t + 1) * P], o_lo[:, axis, c, t * P:(t + 1) * P]),
                                     (wout_hi[:, axis, c, :], wout_lo[:, axis, c, :])) for c in range(CC)],
                                   first=(axis == 1 and t == 0), final=(axis == 0 and t == TT - 1))
                if axis == 0:
                    last.then_inc(y_ready, 1)

            def project_t(b):
                pe.wait_ge(xn_split[1], b + 1)
                for m in range(CC):
                    last = product(t_bank[:, m * TOKENS:(m + 1) * TOKENS],
                                   [((g_hi[:, c, m * P:(m + 1) * P], g_lo[:, c, m * P:(m + 1) * P]),
                                     (xn_hi[1][:, c, :], xn_lo[1][:, c, :])) for c in range(CC)])
                last.then_inc(t_ready, 1)

            def project_row(b):
                for t in range(TT):
                    for c in range(CC):
                        last = pe.matmul(stat_bank[:, 2 * CC + t:2 * CC + t + 1], xn[1][:, c, t * P:(t + 1) * P],
                                         r_col[:, c:c + 1], start=(c == 0), stop=(c == CC - 1))
                last.then_inc(row_ready, 1)

            def project_values(b):
                for t in range(TT):
                    last = product(vp_bank[:, t * DIM:(t + 1) * DIM],
                                   [((xn_hi[1][:, c, t * P:(t + 1) * P], xn_lo[1][:, c, t * P:(t + 1) * P]),
                                     (wvo_hi[:, c, :], wvo_lo[:, c, :])) for c in range(CC)])
                last.then_inc(vp_ready, 1)

            def scores(b, t, s_bank):
                pe.wait_ge(t_lo_done, b + 1)
                if s_bank is vp_bank:
                    pe.wait_ge(vp_lo_done, b + 1)
                product(s_bank[:, t * TOKENS:(t + 1) * TOKENS],
                        [((t_hi[:, c, t * P:(t + 1) * P], t_lo[:, c, t * P:(t + 1) * P]),
                          (xn_hi[1][:, c, :], xn_lo[1][:, c, :])) for c in range(CC)]).then_inc(s_ready, 1)

            def transpose_weights(b):
                pe.wait_ge(attn_ready, b + 1)
                pe.wait_ge(vp_lo_done, b + 1)
                for j in range(TT):
                    for i in range(TT):
                        last = pe.transpose(at_bank[:, (j * TT + i) * P:(j * TT + i + 1) * P],
                                            attn[:, i, j * P:(j + 1) * P], ident[:, :])
                last.then_inc(at_ready, 1)

            def weighted_values(b, i):
                pe.wait_ge(at_lo_done, b + 1)
                product(pv_bank[:, i * DIM:(i + 1) * DIM],
                        [((at_hi[:, j, i, :], at_lo[:, j, i, :]), (vp_hi[:, j, :], vp_lo[:, j, :])) for j in range(TT)]
                        ).then_inc(pv_ready, 1)

            def transpose_x(b):
                pe.wait_ge(x_loaded, 16 * (b + 1))
                transpose_tokens(x_in).then_inc(xt_ready[0], 1)

            def attention(b, has_prev, has_next):
                key_value(b, 0)
                key_value(b, 1)
                if has_prev:
                    pe.wait_ge(xn_ready[1], b)
                if has_next:
                    transpose_x(b + 1)
                if has_prev:
                    project_row(b - 1)
                    project_t(b - 1)
                queries(b, 0)
                if has_prev:
                    pe.wait_ge(row_done, b)
                if has_next:
                    group_mean(0, b + 1)
                if has_prev:
                    if not has_next:
                        pe.wait_ge(out_ready, b - 1)
                    project_values(b - 1)
                key_value(b, 2)
                if has_next:
                    group_variance(0, b + 1)
                queries(b, 1)
                key_value(b, 3)
                if has_prev:
                    scores(b - 1, 0, vp_bank)
                transpose_output(b, 1)
                if has_prev:
                    scores(b - 1, 1, vp_bank)
                queries(b, 2)
                if has_next:
                    project_kv(b + 1, 0)
                if not has_prev:
                    pe.wait_ge(w_split, 3)
                    pe.wait_ge(fold_split, 2)
                project_out(b, 1)
                queries(b, 3)
                if has_next:
                    project_kv(b + 1, 1)
                transpose_output(b, 0)
                if has_next:
                    project_kv(b + 1, 2)
                    project_kv(b + 1, 3)
                project_out(b, 0)

            def project(b, has_prev, has_next):
                if has_next:
                    project_q(b + 1, 0)
                pe.wait_ge(x1_ready, b + 1)
                if has_next:
                    pe.wait_ge(kv_act, ACT_KV * (b + 1) + 1)
                transpose_tokens(x1).then_inc(xt_ready[1], 1)
                if has_prev:
                    transpose_weights(b - 1)
                if has_next:
                    project_q(b + 1, 1)
                group_mean(1, b)
                if has_prev:
                    weighted_values(b - 1, 0)
                group_variance(1, b)
                if has_prev:
                    weighted_values(b - 1, 1)

            pe.wait_ge(consts_ready, 1)
            transpose_x(0)
            group_mean(0, 0)
            group_variance(0, 0)
            pe.wait_ge(l1_loaded, 4 * 16)
            for e in range(CC):
                for o in range(CC):
                    last = pe.transpose(kv_bank[1][:, e * DIM + o * P:e * DIM + (o + 1) * P], wl1[:, 3, o, e * P:(e + 1) * P], ident[:, :])
            last.then_inc(wot_ready, 1)
            for m in range(CC):
                for e in range(CC):
                    last = pe.matmul(y_bank[:, m * DIM:(m + 1) * DIM], wl1[:, 0, e, m * P:(m + 1) * P], wl1[:, 1, e, :],
                                     start=(e == 0), stop=(e == CC - 1))
            last.then_inc(fold_ready, 1)
            pe.wait_ge(w_split, 1)
            project_kv(0, 0)
            project_kv(0, 1)
            pe.wait_ge(w_split, 2)
            project_kv(0, 2)
            project_kv(0, 3)
            project_q(0, 0)
            project_q(0, 1)

            pe.wait_ge(bias_step, 2)
            for i, (weight, vector) in enumerate(((0, 1), (1, 0))):
                for m in range(CC):
                    for e in range(CC):
                        pe.matmul(stat_bank[:, 8 + 2 * i + m:9 + 2 * i + m], wl1[:, weight, e, m * P:(m + 1) * P],
                                  bias_in[:, vector, e:e + 1], start=(e == 0), stop=(e == CC - 1))
            for e in range(CC):
                pe.matmul(stat_bank[:, 12:13], bq_rep[:, e, :], bias_in[:, 1, e:e + 1], start=(e == 0), stop=(e == CC - 1))
            pe.wait_ge(wot_done, 1)
            for e in range(CC):
                last = pe.matmul(kv_bank[0][:, 0:DIM], bv2_rep[:, e, :], wo_t[:, e, :], start=(e == 0), stop=(e == CC - 1))
            last.then_inc(fold_ready, 1)
            pe.wait_ge(fold_split, 1)
            for m in range(CC):
                for e in range(CC):
                    last = pe.matmul(y_bank[:, m * DIM:(m + 1) * DIM], wl1[:, 2, e, m * P:(m + 1) * P], wo_t[:, e, :],
                                     start=(e == 0), stop=(e == CC - 1))
            last.then_inc(fold_ready, 1)
            pe.wait_ge(bias_step, 5)

            attention(0, False, True)
            project(0, False, True)
            with pe.Fori(1, BATCHES - 1) as b:
                attention(b, True, True)
                project(b, True, True)
            attention(BATCHES - 1, True, False)
            project(BATCHES - 1, True, False)
            pe.wait_ge(xn_ready[1], BATCHES)
            project_row(BATCHES - 1)
            project_t(BATCHES - 1)
            pe.wait_ge(out_ready, BATCHES - 1)
            scores(BATCHES - 1, 0, t_bank)
            scores(BATCHES - 1, 1, t_bank)
            project_values(BATCHES - 1)
            transpose_weights(BATCHES - 1)
            weighted_values(BATCHES - 1, 0)
            weighted_values(BATCHES - 1, 1)


_INS = ['x', 'L0_conv_w_qkv0', 'L0_conv_w_out0', 'L0_conv_w_qkv1', 'L0_conv_w_out1', 'L1_conv_Wq', 'L1_conv_bq',
        'L1_conv_Wk', 'L1_conv_bk', 'L1_conv_Wv', 'L1_conv_bv', 'L1_conv_Wo', 'L1_conv_bo', 'L1_conv_sigma']
_OUTS = [((8, 16, 16, 256), 'float32')]


def kernel(**inputs):
    import numpy as _np
    import concourse.bacc as _bacc
    from concourse import mybir as _mybir
    from concourse.bass_utils import run_bass_kernel_spmd as _run

    nc = _bacc.Bacc("TRN2", target_bir_lowering=False, num_devices=1)
    arrays, args = {}, []
    for name in _INS:
        a = _np.ascontiguousarray(inputs[name])
        arrays[f"in_{name}_dram"] = a
        args.append(nc.dram_tensor(f"in_{name}_dram", a.shape, _mybir.dt.from_np(a.dtype), kind="ExternalInput").ap())
    for i, (shape, dtype) in enumerate(_OUTS):
        dt = _mybir.dt.from_np(_np.dtype(dtype))
        args.append(nc.dram_tensor(f"out_{i}_dram", shape, dt, kind="ExternalOutput").ap())
    build(nc, *args)
    r = _run(nc, [arrays], core_ids=[0])
    return r.results[0]["out_0_dram"]
```
